# Optimizing a Trainium2 kernel written in Bass

```python
import numpy as np
import jax
import jax.numpy as jnp

def _softmax(x, axis=-1):
    return jax.nn.softmax(x, axis=axis)

def _gelu(x):
    return jax.nn.gelu(x, approximate=True)

def _silu(x):
    return jax.nn.silu(x)

def _sigmoid(x):
    return jax.nn.sigmoid(x)

def _layernorm(x, axis=-1, eps=1e-05):
    m = jnp.mean(x, axis=axis, keepdims=True)
    v = jnp.var(x, axis=axis, keepdims=True)
    return (x - m) / jnp.sqrt(v + eps)

def _scatter_add(tgt, idx, src, axis=0):
    return tgt.at[idx].add(src)

def _segment_sum(src, seg, n):
    return jax.ops.segment_sum(src, seg, n)
kernel_name = 'mk_seq_preln_d1_jaxref_r4_864439'

def setup_inputs(seed: int=0):
    np.random.seed(seed)
    _w = jnp.asarray

    def _L0_attn_setup():
        import jax, jax.numpy as jnp
        import numpy as np
        EPS = 1e-08

        def elu_feature_map(x):
            return jax.nn.elu(x) + 1.0
        key = jax.random.key(seed)
        ks = jax.random.split(key, 5)
        B, S, D = (2, 1024, 256)
        scale = 1.0 / np.sqrt(D).astype(np.float32)
        x = jax.random.normal(ks[0], (B, S, D), dtype=jnp.float32)
        Wq = jax.random.normal(ks[1], (D, D), dtype=jnp.float32) * scale
        Wk = jax.random.normal(ks[2], (D, D), dtype=jnp.float32) * scale
        Wv = jax.random.normal(ks[3], (D, D), dtype=jnp.float32) * scale
        Wo = jax.random.normal(ks[4], (D, D), dtype=jnp.float32) * scale
        return {'x': x, 'Wq': Wq, 'Wk': Wk, 'Wv': Wv, 'Wo': Wo}
    _L0_attn_in = _L0_attn_setup()

    def _L0_ffn_setup():
        import jax, jax.numpy as jnp
        import numpy as np
        E, H, I = (8, 256, 128)
        NG, TKG, TOPK = (4, 2, 4)
        SCALE = 2.5

        def _mlp(x, wg, wu, wd):
            return jax.nn.silu(x @ wg) * (x @ wu) @ wd
        key = jax.random.key(seed)
        ks = jax.random.split(key, 8)
        s = 0.02
        return {'hidden_states': jax.random.normal(ks[0], (32, 64, H), jnp.float32), 'gate_w': jax.random.normal(ks[1], (E, H), jnp.float32) * np.float32(np.sqrt(2.0 / H)), 'correction_bias': jnp.zeros((E,), jnp.float32), 'Wg': jax.random.normal(ks[2], (E, H, I), jnp.float32) * s, 'Wu': jax.random.normal(ks[3], (E, H, I), jnp.float32) * s, 'Wd': jax.random.normal(ks[4], (E, I, H), jnp.float32) * s, 'Wg_s': jax.random.normal(ks[5], (H, I), jnp.float32) * s, 'Wu_s': jax.random.normal(ks[6], (H, I), jnp.float32) * s, 'Wd_s': jax.random.normal(ks[7], (I, H), jnp.float32) * s}
    _L0_ffn_in = _L0_ffn_setup()
    _d = {'L0_attn_x': _L0_attn_in['x'], 'L0_attn_Wq': _L0_attn_in['Wq'], 'L0_attn_Wk': _L0_attn_in['Wk'], 'L0_attn_Wv': _L0_attn_in['Wv'], 'L0_attn_Wo': _L0_attn_in['Wo'], 'L0_ffn_gate_w': _L0_ffn_in['gate_w'], 'L0_ffn_correction_bias': _L0_ffn_in['correction_bias'], 'L0_ffn_Wg': _L0_ffn_in['Wg'], 'L0_ffn_Wu': _L0_ffn_in['Wu'], 'L0_ffn_Wd': _L0_ffn_in['Wd'], 'L0_ffn_Wg_s': _L0_ffn_in['Wg_s'], 'L0_ffn_Wu_s': _L0_ffn_in['Wu_s'], 'L0_ffn_Wd_s': _L0_ffn_in['Wd_s']}
    _x0 = _d['L0_attn_x']
    _d['L0_attn_x'] = jax.random.normal(jax.random.fold_in(jax.random.key(seed), 1), (16, 512, 256), dtype=_x0.dtype)
    del _x0
    return _d

def reference(L0_attn_x, L0_attn_Wq, L0_attn_Wk, L0_attn_Wv, L0_attn_Wo, L0_ffn_gate_w, L0_ffn_correction_bias, L0_ffn_Wg, L0_ffn_Wu, L0_ffn_Wd, L0_ffn_Wg_s, L0_ffn_Wu_s, L0_ffn_Wd_s):

    def _L0_attn_ref(x, Wq, Wk, Wv, Wo):
        import jax, jax.numpy as jnp
        import numpy as np
        EPS = 1e-08

        def elu_feature_map(x):
            return jax.nn.elu(x) + 1.0
        B, S, D = x.shape
        H = 16
        Dh = D // H

        def proj(W):
            return (x @ W.T).reshape(B, S, H, Dh)
        q = elu_feature_map(proj(Wq))
        k = elu_feature_map(proj(Wk))
        v = proj(Wv)
        q_t = jnp.moveaxis(q, 1, 0)
        k_t = jnp.moveaxis(k, 1, 0)
        v_t = jnp.moveaxis(v, 1, 0)

        def step(carry, qkv):
            kv_sum, k_sum = carry
            q_i, k_i, v_i = qkv
            kv_sum = kv_sum + jnp.einsum('bhd,bhe->bhde', k_i, v_i)
            k_sum = k_sum + k_i
            num = jnp.einsum('bhd,bhde->bhe', q_i, kv_sum)
            den = jnp.sum(q_i * k_sum, axis=-1, keepdims=True)
            out_i = num / (den + EPS)
            return ((kv_sum, k_sum), out_i)
        kv0 = jnp.zeros((B, H, Dh, Dh), dtype=x.dtype)
        ks0 = jnp.zeros((B, H, Dh), dtype=x.dtype)
        _, out = jax.lax.scan(step, (kv0, ks0), (q_t, k_t, v_t))
        out = jnp.moveaxis(out, 0, 1).reshape(B, S, D)
        return out @ Wo.T

    def _L0_ffn_ref(hidden_states, gate_w, correction_bias, Wg, Wu, Wd, Wg_s, Wu_s, Wd_s):
        import jax, jax.numpy as jnp
        import numpy as np
        E, H, I = (8, 256, 128)
        NG, TKG, TOPK = (4, 2, 4)
        SCALE = 2.5

        def _mlp(x, wg, wu, wd):
            return jax.nn.silu(x @ wg) * (x @ wu) @ wd
        B, T, _ = hidden_states.shape
        x = hidden_states.reshape(-1, H)
        N = x.shape[0]
        logits = x @ gate_w.T
        scores = jax.nn.sigmoid(logits)
        scores_c = scores + correction_bias
        grp = scores_c.reshape(N, NG, E // NG)
        group_scores = jnp.sum(jax.lax.top_k(grp, 2)[0], axis=-1)
        grp_idx = jax.lax.top_k(group_scores, TKG)[1]
        group_mask = jnp.zeros_like(group_scores).at[jnp.arange(N)[:, None], grp_idx].set(1.0)
        score_mask = jnp.repeat(group_mask, E // NG, axis=-1) > 0.5
        scores_for_choice = jnp.where(score_mask, scores_c, 0.0)
        topk_idx = jax.lax.top_k(scores_for_choice, TOPK)[1]
        topk_w = jnp.take_along_axis(scores, topk_idx, axis=-1)
        topk_w = topk_w / (jnp.sum(topk_w, axis=-1, keepdims=True) + 1e-20)
        topk_w = topk_w * SCALE
        cw = jnp.sum(jax.nn.one_hot(topk_idx, E, dtype=topk_w.dtype) * topk_w[..., None], axis=1)
        g = jnp.einsum('nh,ehi->eni', x, Wg)
        u = jnp.einsum('nh,ehi->eni', x, Wu)
        y = jnp.einsum('eni,eih->enh', jax.nn.silu(g) * u, Wd)
        routed = jnp.einsum('enh,ne->nh', y, cw)
        out = routed + _mlp(x, Wg_s, Wu_s, Wd_s)
        return out.reshape(B, T, H)
    x = L0_attn_x
    x = x + _L0_attn_ref(_layernorm(x, axis=-1), L0_attn_Wq, L0_attn_Wk, L0_attn_Wv, L0_attn_Wo)
    x = x + _L0_ffn_ref(_layernorm(x, axis=-1), L0_ffn_gate_w, L0_ffn_correction_bias, L0_ffn_Wg, L0_ffn_Wu, L0_ffn_Wd, L0_ffn_Wg_s, L0_ffn_Wu_s, L0_ffn_Wd_s)
    return x

_drawn_inputs = setup_inputs


def setup_inputs(seed=0):
    import zlib

    import numpy as np

    out = dict(_drawn_inputs(seed))
    spreads = {'L0_ffn_correction_bias': (0.0, 0.8)}
    factors = {'L0_attn_Wq': 4.311,
     'L0_ffn_gate_w': 4.889,
     'L0_ffn_Wg': 3.602,
     'L0_ffn_Wu': 3.56,
     'L0_ffn_Wd': 3.563,
     'L0_ffn_Wg_s': 4.876,
     'L0_ffn_Wu_s': 4.775,
     'L0_ffn_Wd_s': 4.799}
    for name, (base, spread) in spreads.items():
        noise = np.random.default_rng([zlib.crc32(name.encode()), seed]).standard_normal(out[name].shape)
        drawn = base * np.exp(spread * noise) if base else spread * noise
        out[name] = jnp.asarray(drawn.astype(out[name].dtype))
    for name, factor in factors.items():
        out[name] = (out[name] * factor).astype(out[name].dtype)
    return out
```

```python
import concourse.bass as bass
from concourse import mybir
from contextlib import ExitStack
import numpy as np

B, S, D = 16, 512, 256
H, DH = 16, 16
E, FF = 8, 128
GROUPS, TOP_GROUPS, TOP_K = 4, 2, 4
ROUTE_SCALE = 2.5
LN_EPS, ATT_EPS, ROUTE_EPS = 1e-5, 1e-8, 1e-20

P = 128
SUBS = S // P
KC = D // P
MH = P // DH
VW = DH + 1
PER_G = E // GROUPS
SLOTS = E + 1

ET, HR, CW, SM, GB = 3, 3, 4, 8, 3

def score_parts(m, half):
    out = [("state", m * SUBS + c) for c in (2 * half, 2 * half + 1) if c]
    return out + [("scores", 4 * (2 * m + half) + g) for g in range(4)]


def value_parts(m, half):
    return [("values", 2 * m + half)]


SCHEDULE = (
    [("ln1_stats", 0), ("gate", 0), ("up", 0), ("ln1_apply", 0), ("split", 0), ("gate", 1), ("up", 1),
     ("turn", 0), ("turn", 1), ("split", 1), ("down", 0), ("gate", 2),
     ("v", 0), ("k", 0), ("v", 1), ("q", 0), ("k_split", 0), ("up", 2), ("k_turn", 0),
     ("q_split", 0), ("k", 1), ("split", 2), ("q", 1), ("down", 1), ("k_split", 1), ("q_split", 1), ("k_turn", 1)]
    + score_parts(0, 0) + [("gate", 3)] + value_parts(0, 0) + [("up", 3)]
    + score_parts(0, 1) + [("down", 2), ("split", 3)] + value_parts(0, 1) + [("gate", 4)]
    + score_parts(1, 0) + [("up", 4)] + value_parts(1, 0) + [("split", 4), ("down", 3)]
    + score_parts(1, 1) + [("gate", 5)] + value_parts(1, 1) + [("up", 5), ("down", 4), ("split", 5), ("gate", 6)]
    + [("turn", 2), ("turn", 3), ("up", 6), ("down", 5), ("wo", 0), ("wo", 1), ("split", 6), ("ln2_stats", 0),
       ("gate", 7), ("up", 7), ("ln2_apply", 0), ("split", 7), ("down", 6),
       ("turn", 4), ("turn", 5), ("gate", 8), ("router", 0), ("up", 8), ("route", 0), ("split", 8),
       ("down", 7), ("down", 8), ("weights_turn", 0), ("result", 0)]
)
EXPERT_PARTS = ("gate", "up", "split", "down", "result")
ATTENTION = [x for x in SCHEDULE if x[0] not in EXPERT_PARTS]
EXPERTS = [x for x in SCHEDULE if x[0] in EXPERT_PARTS]
BANKED = ("turn", "v", "k", "q", "k_turn", "state", "scores", "wo", "router", "weights_turn")
USE = {x: n for n, x in enumerate(x for x in SCHEDULE if x[0] in BANKED)}
USES = len(USE)
assert USES % 2 == 0


def linear_attention_moe(nc, x, w_qkvo, w_gate_up, w_down, w_router, bias, consts, out):
    f32, f32r = mybir.dt.float32, mybir.dt.float32r
    ALU, ACT, AX = mybir.AluOpType, mybir.ActivationFunctionType, mybir.AxisListType

    ctx = ExitStack()
    with ctx:
        def sb(name, shape, dt=f32):
            return ctx.enter_context(nc.sbuf_tensor(name, shape, dt))

        def ps(name, shape):
            return ctx.enter_context(nc.psum_tensor(name, shape, f32))

        def sem(name):
            return ctx.enter_context(nc.semaphore(name))

        wa_hi, wa_lo = (sb(f"wa_{n}", [P, KC, 4 * D], f32r) for n in ("hi", "lo"))
        wg_hi, wg_lo = (sb(f"wg_{n}", [P, SLOTS, 2, KC, FF], f32r) for n in ("hi", "lo"))
        wd_hi, wd_lo = (sb(f"wd_{n}", [P, SLOTS, D], f32r) for n in ("hi", "lo"))
        wr_parts = sb("wr_parts", [P, KC, 2, E], f32r)
        wr_raw = sb("wr_raw", [P, KC, E])
        bias_sb = sb("bias_sb", [P, E])
        cst = sb("cst", [P, CONST_COLS])
        ident = cst[:, C_IDENT:C_IDENT + P]
        causal = cst[:, C_CAUSAL:C_CAUSAL + P]
        block_mask = cst[:, C_BLOCK:C_BLOCK + MH * VW]
        before_e = cst[:, C_TIE_E:C_TIE_E + E * E].rearrange("p (a b) -> p a b", a=E)
        before_g = cst[:, C_TIE_G:C_TIE_G + GROUPS * GROUPS].rearrange("p (a b) -> p a b", a=GROUPS)
        power = cst[:, C_POW:C_POW + SUBS]

        x_in = sb("x_in", [P, SUBS, D])
        x_mid = [sb(f"x_mid{i}", [P, SUBS, D]) for i in range(2)]
        norm = sb("norm", [P, SUBS, D])
        at_hi, at_lo = (sb(f"at_{n}", [P, KC, S], f32r) for n in ("hi", "lo"))
        xt_hi, xt_lo = ([sb(f"xt_{n}{i}", [P, KC, S], f32r) for i in range(2)] for n in ("hi", "lo"))
        kf, qf = sb("kf", [P, KC, S]), sb("qf", [P, KC, S])
        expo = sb("expo", [P, 2, S])
        k_hi, k_lo = (sb(f"k_{n}", [P, KC, S], f32r) for n in ("hi", "lo"))
        q_hi, q_lo = (sb(f"q_{n}", [P, KC, 2, S], f32r) for n in ("hi", "lo"))
        k_tok = sb("k_tok", [P, KC, SUBS - 1, P])
        v_aug = sb("v_aug", [P, SUBS, H, VW])
        scores = sb("scores", [P, SM, 4, P])
        stage = scores[:, :, :, :].rearrange("p (a s) h q -> p a (s h q)", a=2)
        st = sb("st", [P, 2, MH * VW])
        st_new = sb("st_new", [P, MH * VW])
        den = sb("den", [P, 2, MH])
        rden = sb("rden", [P, 2, MH])
        stats = sb("stats", [P, SUBS, 6])
        m_sum, m_dif, v_sum, mean = (sb(n, [P, SUBS]) for n in ("m_sum", "m_dif", "v_sum", "mean"))
        veps = sb("veps", [P, SUBS])
        rstd = sb("rstd", [P, SUBS])
        logit = sb("logit", [P, SUBS, E])
        sig = sb("sig", [P, SUBS, E])
        sig_c = sb("sig_c", [P, SUBS, E])
        g_sum = sb("g_sum", [P, SUBS, GROUPS])
        g_cmp = sb("g_cmp", [P, SUBS, GROUPS, 2, GROUPS])
        g_eq = sb("g_eq", [P, SUBS, GROUPS, GROUPS])
        g_rank = sb("g_rank", [P, SUBS, GROUPS])
        choice = sb("choice", [P, SUBS, E])
        e_cmp = sb("e_cmp", [P, SUBS, E, 2, E])
        e_eq = sb("e_eq", [P, SUBS, E, E])
        e_rank = sb("e_rank", [P, SUBS, E])
        w_sel = sb("w_sel", [P, SUBS, E])
        w_sum = sb("w_sum", [P, SUBS])
        w_rec = sb("w_rec", [P, SUBS])
        cw = sb("cw", [P, E, SUBS])
        cw_t = sb("cw_t", [E * SUBS, P])
        cw_all = sb("cw_all", [P, CW, S])
        et = sb("et", [P, ET, S])
        h_hi, h_lo = (sb(f"h_{n}", [P, HR, S], f32r) for n in ("hi", "lo"))

        bank = [ps(f"bank{i}", [P, S]) for i in range(2)]
        o_bank = ps("o_bank", [P, 2, MH * VW])
        g_bank = [ps(f"g_bank{i}", [P, S]) for i in range(GB)]
        y_bank = [ps(f"y_bank{i}", [P, 2, D]) for i in range(2)]
        cw_dram = nc.dram_tensor("cw_dram", [2, E, S], f32, kind="Internal").ap()

        x_v = x.rearrange("b (s p) d -> b p s d", p=P)
        out_v = out.rearrange("b (s p) d -> b p s d", p=P)

        staged = [sem(f"staged{i}") for i in range(2)]
        small_in = sem("small_in")
        split_hi = sem("split_hi")
        split_lo = sem("split_lo")
        ones_set = sem("ones_set")
        x_loaded = sem("x_loaded")
        filled = sem("filled")
        drained = [sem(f"drained{i}") for i in range(2)]
        turn_hi = sem("turn_hi")
        exp_done = sem("exp_done")
        relu_done = sem("relu_done")
        k_hi_done, k_lo_done = sem("k_hi_done"), sem("k_lo_done")
        q_hi_done, q_lo_done = sem("q_hi_done"), sem("q_lo_done")
        state_done = sem("state_done")
        o_filled = sem("o_filled")
        heads_done = sem("heads_done")
        var_ready, rstd_ready = sem("var_ready"), sem("rstd_ready")
        norm_ready = sem("norm_ready")
        expn_done = sem("expn_done")
        cw_ready = sem("cw_ready")
        cw_stored = sem("cw_stored")
        cw_loaded = [sem(f"cw_loaded{i}") for i in range(CW)]
        cw_used = sem("cw_used")
        g_filled = sem("g_filled")
        g_drained = sem("g_drained")
        tanh_done = sem("tanh_done")
        h_hi_done, h_lo_done = sem("h_hi_done"), sem("h_lo_done")
        down_done = sem("down_done")
        y_drained = sem("y_drained")
        out_sent = [sem(f"out_sent{i}") for i in range(2)]
        chain_a, chain_e = sem("chain_a"), sem("chain_e")

        def wait(eng, s, value):
            if isinstance(value, int) and value <= 0:
                return
            eng.wait_ge(s, value)

        def wait_filled(eng, b, part):
            eng.wait_ge(filled, USES * b + USE[part] + 1)

        def wait_drained(eng, b, *parts, fill=None):
            need = [0, 0]
            for part in parts:
                n = USE[part]
                need[n % 2] = max(need[n % 2], n // 2 + 1)
            if fill:
                n = USE[fill]
                need[n % 2] = max(need[n % 2], n // 2)
            for j in range(2):
                if need[j] or (fill and USE[fill] % 2 == j):
                    wait(eng, drained[j], USES // 2 * b + need[j])

        def bank_of(part):
            return bank[USE[part] % 2]

        def run(step, eng):
            step(ATTENTION, -1, -1, 1)
            step(SCHEDULE, 0, 0, 0)
            with eng.Fori(0, (B - 2) // 2) as k:
                step(SCHEDULE, k * 2 + 1, k, 1)
                step(SCHEDULE, k * 2 + 2, k + 1, 0)
            step(EXPERTS, B - 1, (B - 1) // 2, 1)

        PIECES = []
        for kc in range(KC):
            PIECES.append((w_qkvo[:, kc], 4 * D, wa_hi[:, kc], wa_lo[:, kc]))
        GU = 2 * KC * FF
        for s in range(0, SLOTS, 2):
            n = min(2, SLOTS - s)
            PIECES.append((w_gate_up[:, s * GU:(s + n) * GU], n * GU,
                           wg_hi[:, s:s + n].rearrange("p s g k f -> p (s g k f)"),
                           wg_lo[:, s:s + n].rearrange("p s g k f -> p (s g k f)")))
        for s in range(0, SLOTS, 4):
            n = min(4, SLOTS - s)
            PIECES.append((w_down[:, s * D:(s + n) * D], n * D,
                           wd_hi[:, s:s + n].rearrange("p s n -> p (s n)"),
                           wd_lo[:, s:s + n].rearrange("p s n -> p (s n)")))
        NP = len(PIECES)
        block = ctx.enter_context(nc.Block())

        @block.sync
        def _(sp):
            def load_x(b):
                sp.dma_start(x_in[:, :, :], x_v[b] if isinstance(b, int) else
                             x_v[bass.ds(b, 1)].rearrange("a p s d -> p (a s) d")).then_inc(x_loaded, 16)

            load_x(0)
            sp.dma_start(cst[:, :], consts).then_inc(small_in, 16)
            sp.dma_start(bias_sb[:, :], bias.partition_broadcast(P)).then_inc(small_in, 16)
            sp.dma_start(wr_raw[:, :, :], w_router).then_inc(small_in, 16)
            for n, (src, cols, _, _) in enumerate(PIECES):
                if n >= 2:
                    sp.wait_ge(split_lo, n - 1)
                sp.dma_start(stage[:, n % 2, 0:cols], src).then_inc(staged[n % 2], 16)

            def step(parts, b, half, parity):
                a, pa = b + 1, 1 - parity
                if parts is not ATTENTION:
                    for e in range(4):
                        load_cw(b, parity, e)
                for name, i in parts:
                    if name == "down" and i < E - CW:
                        load_cw(b, parity, i + CW)
                    elif name == "ln2_stats":
                        wait_drained(sp, a, ("wo", 1))
                        next_x(a)
                    elif name == "weights_turn":
                        wait_drained(sp, a, ("weights_turn", 0))
                        sp.dma_start(cw_dram[pa].rearrange("e (s p) -> (e s) p", p=P), cw_t[:, :])\
                            .then_inc(cw_stored, 16)
                    elif name == "result":
                        sp.wait_ge(y_drained, 2 * b + 2)
                        sp.dma_start(out_v[b] if isinstance(b, int) else
                                     out_v[bass.ds(b, 1)].rearrange("a p s d -> p (a s) d"),
                                     x_mid[parity][:, :, :]).then_inc(out_sent[parity], 16)

            def next_x(a):
                load_x((a + 1) % B)

            def load_cw(b, parity, e):
                if e == 0:
                    sp.wait_ge(cw_stored, 16 * b + 16)
                wait(sp, cw_used, E * b + e - CW + 1)
                sp.dma_start(cw_all[:, e % CW, :], cw_dram[parity, e].partition_broadcast(P))\
                    .then_inc(cw_loaded[e % CW], 16)

            run(step, sp)
            sp.wait_ge(out_sent[0], 16 * (B // 2))
            sp.wait_ge(out_sent[1], 16 * (B // 2))
            sp.wait_ge(x_loaded, 16 * (B + 1))

        @block.scalar
        def _(act):
            for n, (_, cols, hi, _) in enumerate(PIECES):
                act.wait_ge(staged[n % 2], 16 * (n // 2 + 1))
                nc.scalar.activation(hi, stage[:, n % 2, 0:cols], ACT.Copy).then_inc(split_hi, 1)
            act.wait_ge(small_in, 48)
            nc.scalar.activation(wr_parts[:, :, 0, :], wr_raw[:, :, :], ACT.Copy).then_inc(split_hi, 1)

            def step(parts, b, half, parity):
                a, pa = b + 1, 1 - parity

                def h_high(e):
                    if e == 0:
                        act.wait_ge(g_drained, 2 * SLOTS * b + 2)
                    else:
                        act.wait_ge(cw_used, E * b + e)
                    wait(act, down_done, SLOTS * b + e - HR + 1)
                    nc.scalar.activation(h_hi[:, e % HR, :], et[:, e % ET, :], ACT.Copy)\
                        .then_inc(h_hi_done, 1)

                for name, i in parts:
                    part = (name, i)
                    if name == "gate":
                        act.wait_ge(g_filled, 2 * SLOTS * b + 2 * i + 1)
                        wait(act, h_lo_done, SLOTS * b + i - ET + 1)
                        nc.scalar.activation(et[:, i % ET, :], g_bank[2 * i % GB][:, :], ACT.Tanh,
                                             scale=0.5).then_inc(tanh_done, 1)
                    elif name == "split":
                        h_high(i)
                    elif name == "turn":
                        wait_filled(act, a, part)
                        dst = at_hi if i < 4 else xt_hi[pa]
                        nc.scalar.activation(dst[:, i % 2, :], bank_of(part)[:, :], ACT.Copy)\
                            .then_inc(turn_hi, 1)
                    elif name == "v":
                        if i == 0:
                            act.wait_ge(ones_set, 1)
                        wait_filled(act, a, part)
                        nc.scalar.activation(v_aug[:, 2 * i:2 * i + 2, :, 0:DH],
                                             bank_of(part)[:, :].rearrange("p (s h d) -> p s h d", s=2, h=H),
                                             ACT.Copy).then_inc(drained[USE[part] % 2], 1)
                    elif name in ("k", "q"):
                        n = 2 * i + (name == "q")
                        wait_filled(act, a, part)
                        if n >= 2:
                            wait_drained(act, a, (name, i - 1))
                        else:
                            wait(act, drained[USE[(name, 1)] % 2], USES // 2 * (a - 1) + USE[(name, 1)] // 2 + 1)
                        nc.scalar.activation(expo[:, n % 2, :], bank_of(part)[:, :], ACT.Relu, scale=-1.0)\
                            .then_inc(relu_done, 1)
                        act.wait_ge(relu_done, 4 * a + n + 1)
                        nc.scalar.activation(expo[:, n % 2, :], expo[:, n % 2, :], ACT.Exp, scale=-1.0)\
                            .then_inc(exp_done, 1)
                    elif name == "k_split":
                        wait_drained(act, a, ("k", i))
                        nc.scalar.activation(k_hi[:, i, :], kf[:, i, :], ACT.Copy).then_inc(k_hi_done, 1)
                    elif name == "q_split":
                        wait_drained(act, a, ("q", i))
                        for j in range(2):
                            nc.scalar.activation(q_hi[:, i, j, :], qf[:, i, :], ACT.Copy,
                                                 scale=cst[:, C_EO + j:C_EO + j + 1]).then_inc(q_hi_done, 1)
                    elif name == "k_turn":
                        wait_filled(act, a, part)
                        nc.scalar.activation(k_tok[:, i, :, :].rearrange("p c d -> p (c d)"),
                                             bank_of(part)[:, 0:(SUBS - 1) * P], ACT.Copy)\
                            .then_inc(drained[USE[part] % 2], 1)
                    elif name == "route":
                        wait_drained(act, a, ("router", 0))
                        nc.scalar.activation(sig[:, :, :], logit[:, :, :], ACT.Exp, scale=-1.0)\
                            .then_inc(expn_done, 1)
                    elif name == "weights_turn":
                        wait_filled(act, a, part)
                        wait(act, cw_stored, 16 * a)
                        nc.scalar.activation(cw_t[:, :], bank_of(part)[0:E * SUBS, 0:P], ACT.Copy)\
                            .then_inc(drained[USE[part] % 2], 1)

            run(step, act)

        @block.gpsimd
        def _(pool):
            nc.gpsimd.memset(v_aug[:, :, :, DH:VW], 1.0).then_inc(ones_set, 1)

            def step(parts, b, half, parity):
                a = b + 1

                def weigh(e):
                    if e == 0:
                        return
                    r = (e - 1) % CW
                    pool.wait_ge(cw_loaded[r], 16 * (E // CW * b + (e - 1) // CW + 1))
                    pool.wait_ge(g_drained, 2 * SLOTS * b + 2 * e + 2)
                    nc.gpsimd.tensor_tensor(et[:, e % ET, :], et[:, e % ET, :], cw_all[:, r, :], ALU.mult)\
                        .then_inc(cw_used, 1)

                def h_low(e):
                    pool.wait_ge(h_hi_done, SLOTS * b + e + 1)
                    nc.gpsimd.tensor_tensor(h_lo[:, e % HR, :], et[:, e % ET, :],
                                            h_hi[:, e % HR, :].bitcast(f32), ALU.subtract)\
                        .then_inc(h_lo_done, 1)

                for name, i in parts:
                    if name == "up":
                        weigh(i)
                    elif name == "split":
                        h_low(i)
                    elif name in ("ln1_apply", "ln2_apply"):
                        n = 2 * a + (name == "ln2_apply")
                        pool.wait_ge(var_ready, n + 1)
                        nc.gpsimd.tensor_tensor(rstd[:, :], veps[:, :], power, ALU.pow)\
                            .then_inc(rstd_ready, 1)

            run(step, pool)

        @block.vector
        def _(dve):
            for n, (_, cols, hi, lo) in enumerate(PIECES):
                dve.wait_ge(split_hi, n + 1)
                nc.vector.tensor_tensor(lo, stage[:, n % 2, 0:cols], hi.bitcast(f32), ALU.subtract)\
                    .then_inc(split_lo, 1)
            dve.wait_ge(split_hi, NP + 1)
            nc.vector.tensor_tensor(wr_parts[:, :, 1, :], wr_raw[:, :, :],
                                    wr_parts[:, :, 0, :].bitcast(f32), ALU.subtract).then_inc(split_lo, 1)

            def step(parts, b, half, parity):
                a, pa = b + 1, 1 - parity
                own = [0]

                def link(ins):
                    own[0] += 1
                    ins.then_inc(chain_a, 1)
                    dve.wait_ge(chain_a, CHAIN_A * a + own[0])

                def layernorm_stats(src):
                    for s in range(SUBS):
                        last = nc.vector.bn_stats(stats[:, s, :], src[:, s, :])
                    link(last)
                    m0, m1, v0, v1 = (stats[:, :, j] for j in (1, 4, 2, 5))
                    nc.vector.tensor_tensor(m_sum[:, :], m0, m1, ALU.add)
                    nc.vector.tensor_tensor(m_dif[:, :], m0, m1, ALU.subtract)
                    link(nc.vector.tensor_tensor(v_sum[:, :], v0, v1, ALU.add))
                    nc.vector.tensor_scalar(mean[:, :], m_sum[:, :], 0.5, None, ALU.mult)
                    nc.vector.scalar_tensor_tensor(m_dif[:, :], m_dif[:, :], 0.25, m_dif[:, :],
                                                   ALU.mult, ALU.mult)
                    link(nc.vector.tensor_scalar(v_sum[:, :], v_sum[:, :], 1.0 / D, LN_EPS, ALU.mult, ALU.add))
                    nc.vector.tensor_tensor(veps[:, :], m_dif[:, :], v_sum[:, :], ALU.add)\
                        .then_inc(var_ready, 1)

                def layernorm_apply(src, n):
                    dve.wait_ge(rstd_ready, n)
                    for s in range(SUBS):
                        last = nc.vector.tensor_scalar(norm[:, s, :], src[:, s, :], mean[:, s:s + 1],
                                                       rstd[:, s:s + 1], ALU.subtract, ALU.mult)
                    last.then_inc(norm_ready, 1)

                def beaten(values, n, cmp, eq, before, rank):
                    other = values.unsqueeze(2).broadcast_to([P, SUBS, n, n])
                    own_v = values.unsqueeze(3).broadcast_to([P, SUBS, n, n])
                    nc.vector.tensor_tensor(cmp[:, :, :, 0, :], other, own_v, ALU.is_gt)
                    link(nc.vector.tensor_tensor(eq[:, :, :, :], other, own_v, ALU.is_equal))
                    link(nc.vector.tensor_tensor(cmp[:, :, :, 1, :], eq[:, :, :, :],
                                                 before.unsqueeze(1).broadcast_to([P, SUBS, n, n]),
                                                 ALU.mult))
                    link(nc.vector.tensor_reduce(rank[:, :, :],
                                                 cmp[:, :, :, :, :].rearrange("p s a t b -> p (s a) (t b)"),
                                                 AX.X, ALU.add))

                for name, i in parts:
                    part = (name, i)
                    if name == "gate":
                        dve.wait_ge(tanh_done, SLOTS * b + i + 1)
                        nc.vector.scalar_tensor_tensor(et[:, i % ET, :], et[:, i % ET, :], 1.0,
                                                       g_bank[2 * i % GB][:, :], ALU.add, ALU.mult)\
                            .then_inc(g_drained, 1)
                    elif name == "up":
                        dve.wait_ge(g_filled, 2 * SLOTS * b + 2 * i + 2)
                        dve.wait_ge(g_drained, 2 * SLOTS * b + 2 * i + 1)
                        nc.vector.scalar_tensor_tensor(et[:, i % ET, :], et[:, i % ET, :], 0.5,
                                                       g_bank[(2 * i + 1) % GB][:, :], ALU.mult, ALU.mult)\
                            .then_inc(g_drained, 1)
                    elif name == "result":
                        dve.wait_ge(down_done, SLOTS * b + SLOTS)
                        for j in range(2):
                            xm = x_mid[parity][:, 2 * j:2 * j + 2, :]
                            nc.vector.tensor_tensor(xm, xm, y_bank[j][:, :, :], ALU.add)\
                                .then_inc(y_drained, 1)
                    elif name == "ln1_stats":
                        dve.wait_ge(x_loaded, 16 * a + 16)
                        layernorm_stats(x_in)
                    elif name == "ln1_apply":
                        layernorm_apply(x_in, 2 * a + 1)
                    elif name == "ln2_stats":
                        wait_drained(dve, a, ("wo", 0), ("wo", 1))
                        layernorm_stats(x_mid[pa])
                    elif name == "ln2_apply":
                        layernorm_apply(x_mid[pa], 2 * a + 2)
                    elif name == "turn":
                        dve.wait_ge(turn_hi, 6 * a + i + 1)
                        dst, hi = (at_lo, at_hi) if i < 4 else (xt_lo[pa], xt_hi[pa])
                        nc.vector.tensor_tensor(dst[:, i % 2, :], bank_of(part)[:, :],
                                                hi[:, i % 2, :].bitcast(f32), ALU.subtract)\
                            .then_inc(drained[USE[part] % 2], 1)
                    elif name in ("k", "q"):
                        n = 2 * i + (name == "q")
                        dve.wait_ge(exp_done, 4 * a + n + 1)
                        dst = kf if name == "k" else qf
                        nc.vector.scalar_tensor_tensor(dst[:, i, :], bank_of(part)[:, :], 0.0,
                                                       expo[:, n % 2, :], ALU.max, ALU.add)\
                            .then_inc(drained[USE[part] % 2], 1)
                    elif name == "k_split":
                        dve.wait_ge(k_hi_done, 2 * a + i + 1)
                        nc.vector.tensor_tensor(k_lo[:, i, :], kf[:, i, :], k_hi[:, i, :].bitcast(f32),
                                                ALU.subtract).then_inc(k_lo_done, 1)
                    elif name == "q_split":
                        for j in range(2):
                            dve.wait_ge(q_hi_done, 4 * a + 2 * i + j + 1)
                            nc.vector.scalar_tensor_tensor(q_lo[:, i, j, :], qf[:, i, :],
                                                           cst[:, C_EO + j:C_EO + j + 1],
                                                           q_hi[:, i, j, :].bitcast(f32),
                                                           ALU.mult, ALU.subtract).then_inc(q_lo_done, 1)
                    elif name == "state":
                        c = i % SUBS
                        wait_filled(dve, a, part)
                        dst = st[:, 1, :] if c == 1 else st_new[:, :]
                        if c > 1:
                            wait(dve, state_done, 4 * a + 2 * (i // SUBS) + c - 2)
                        nc.vector.tensor_tensor(dst, bank_of(part)[:, 0:MH * VW], block_mask, ALU.mult)\
                            .then_inc(drained[USE[part] % 2], 1)
                        if c > 1:
                            wait_drained(dve, a, part)
                            nc.vector.tensor_tensor(st[:, c % 2, :], st[:, (c - 1) % 2, :], st_new[:, :],
                                                    ALU.add).then_inc(state_done, 1)
                    elif name == "scores":
                        wait_filled(dve, a, part)
                        wait(dve, o_filled, 4 * a + (i - SM) // 4 + 1)
                        nc.vector.tensor_tensor(scores[:, i % SM, :, :],
                                                bank_of(part)[:, :].rearrange("p (h q) -> p h q", h=4),
                                                causal.unsqueeze(1).broadcast_to([P, 4, P]), ALU.mult)\
                            .then_inc(drained[USE[part] % 2], 1)
                    elif name == "values":
                        m, c = i // 2, 2 * (i % 2)
                        o = o_bank[:, :, :].rearrange("p c (h d) -> p c h d", h=MH)
                        dve.wait_ge(o_filled, 4 * a + i + 1)
                        link(nc.vector.tensor_scalar(den[:, :, :], o[:, :, :, DH], ATT_EPS, None, ALU.add))
                        link(nc.vector.reciprocal(rden[:, :, :], den[:, :, :]))
                        nc.vector.tensor_tensor(
                            norm[:, c:c + 2, m * P:(m + 1) * P].rearrange("p c (h d) -> p c h d", h=MH),
                            o[:, :, :, 0:DH], rden[:, :, :].unsqueeze(3).broadcast_to([P, 2, MH, DH]),
                            ALU.mult).then_inc(heads_done, 1)
                    elif name == "wo":
                        wait_filled(dve, a, part)
                        if i == 0:
                            wait(dve, out_sent[pa], 16 * half_of(b, half, parity))
                        nc.vector.tensor_tensor(x_mid[pa][:, 2 * i:2 * i + 2, :],
                                                bank_of(part)[:, :].rearrange("p (s d) -> p s d", s=2),
                                                x_in[:, 2 * i:2 * i + 2, :], ALU.add)\
                            .then_inc(drained[USE[part] % 2], 1)
                    elif name == "router":
                        wait_filled(dve, a, part)
                        nc.vector.tensor_reduce(
                            logit[:, :, :].rearrange("p s e -> p (s e)"),
                            bank_of(part)[:, 0:SUBS * 2 * E].rearrange("p (s t e) -> p s e t", s=SUBS, t=2),
                            AX.X, ALU.add).then_inc(drained[USE[part] % 2], 1)
                    elif name == "route":
                        dve.wait_ge(expn_done, a + 1)
                        link(nc.vector.tensor_scalar(sig_c[:, :, :], sig[:, :, :], 1.0, None, ALU.add))
                        link(nc.vector.reciprocal(sig[:, :, :], sig_c[:, :, :]))
                        link(nc.vector.tensor_tensor(sig_c[:, :, :], sig[:, :, :],
                                                     bias_sb[:, :].unsqueeze(1).broadcast_to([P, SUBS, E]), ALU.add))
                        pair = sig_c[:, :, :].rearrange("p s (g t) -> p s g t", t=PER_G)
                        link(nc.vector.tensor_tensor(g_sum[:, :, :], pair[:, :, :, 0], pair[:, :, :, 1], ALU.add))
                        beaten(g_sum[:, :, :], GROUPS, g_cmp, g_eq, before_g, g_rank)
                        link(nc.vector.tensor_scalar(g_rank[:, :, :], g_rank[:, :, :], TOP_GROUPS - 0.5, None,
                                                     ALU.is_lt))
                        link(nc.vector.tensor_tensor(choice[:, :, :].rearrange("p s (g t) -> p s g t", t=PER_G), pair,
                                                     g_rank[:, :, :].unsqueeze(3)
                                                     .broadcast_to([P, SUBS, GROUPS, PER_G]), ALU.mult))
                        beaten(choice[:, :, :], E, e_cmp, e_eq, before_e, e_rank)
                        link(nc.vector.scalar_tensor_tensor(w_sel[:, :, :], e_rank[:, :, :], TOP_K - 0.5,
                                                            sig[:, :, :], ALU.is_lt, ALU.mult))
                        link(nc.vector.tensor_reduce(w_sum[:, :], w_sel[:, :, :], AX.X, ALU.add))
                        link(nc.vector.tensor_scalar(w_sum[:, :], w_sum[:, :], ROUTE_EPS, None, ALU.add))
                        link(nc.vector.reciprocal(w_rec[:, :], w_sum[:, :]))
                        nc.vector.scalar_tensor_tensor(cw[:, :, :].rearrange("p e s -> p s e"), w_sel[:, :, :],
                                                       ROUTE_SCALE,
                                                       w_rec[:, :].unsqueeze(2).broadcast_to([P, SUBS, E]),
                                                       ALU.mult, ALU.mult).then_inc(cw_ready, 1)
                if parts is not EXPERTS:
                    assert own[0] == CHAIN_A, own[0]

            def half_of(b, half, parity):
                return half + 1 if parity == 1 else half

            run(step, dve)

        @block.tensor
        def _(pe):
            def product(dst, lhs, rhs, first, last, shared=False):
                (lh, ll), (rh, rl) = lhs, rhs
                for n, (l, r) in enumerate(((lh, rh), (lh, rl), (ll, rh))):
                    ins = nc.tensor.matmul(dst, l, r, start=first and n == 0, stop=last and n == 2,
                                           skip_group_check=shared)
                return ins

            def cols(parts, *index):
                return tuple(p[index] for p in parts)

            WA, WG, WD = (wa_hi, wa_lo), (wg_hi, wg_lo), (wd_hi, wd_lo)
            AT = (at_hi, at_lo)
            ALL = slice(None)

            def step(parts, b, half, parity):
                a, pa = b + 1, 1 - parity
                XT, XA = (xt_hi[parity], xt_lo[parity]), (xt_hi[pa], xt_lo[pa])
                for name, i in parts:
                    part = (name, i)
                    if name in BANKED:
                        bk = bank_of(part)
                    if name in ("gate", "up"):
                        n = 2 * i + (name == "up")
                        if i == 0 and name == "gate":
                            wait_drained(pe, b, ("turn", 5))
                        wait(pe, g_drained, 2 * SLOTS * b + n - GB + 1)
                        if isinstance(b, int) and b == 0:
                            pe.wait_ge(split_lo, KC + i // 2 + 1)
                        for kc in range(KC):
                            last = product(g_bank[n % GB][:, :], cols(WG, ALL, i, n % 2, kc, ALL),
                                           cols(XT, ALL, kc, ALL), kc == 0, kc == KC - 1)
                        last.then_inc(g_filled, 1)
                    elif name == "down":
                        pe.wait_ge(h_lo_done, SLOTS * b + i + 1)
                        if i == 0:
                            wait(pe, y_drained, 2 * b)
                        if isinstance(b, int) and b == 0:
                            pe.wait_ge(split_lo, KC + (SLOTS + 1) // 2 + i // 4 + 1)
                        for s in range(SUBS):
                            last = product(y_bank[s // 2][:, s % 2, :],
                                           (h_hi[:, i % HR, s * P:(s + 1) * P], h_lo[:, i % HR, s * P:(s + 1) * P]),
                                           cols(WD, ALL, i, ALL), i == 0 and s % 2 == 0, i == SLOTS - 1, shared=True)
                        last.then_inc(down_done, 1)
                    elif name == "turn":
                        if i == 0:
                            if isinstance(a, int) and a == 0:
                                pe.wait_ge(small_in, 48)
                            pe.wait_ge(norm_ready, 2 * a + 1)
                        elif i in (2, 3):
                            pe.wait_ge(heads_done, 4 * a + 4)
                        elif i == 4:
                            pe.wait_ge(norm_ready, 2 * a + 2)
                        wait_drained(pe, a, fill=part)
                        for s in range(SUBS):
                            last = nc.tensor.transpose(bk[:, s * P:(s + 1) * P],
                                                       norm[:, s, (i % 2) * P:(i % 2 + 1) * P], ident)
                        last.then_inc(filled, 1)
                    elif name in ("v", "wo"):
                        if name == "v":
                            wait_drained(pe, a, ("turn", 0), ("turn", 1), fill=part)
                            if isinstance(a, int) and a == 0:
                                pe.wait_ge(split_lo, KC)
                        else:
                            wait_drained(pe, a, ("turn", 2), ("turn", 3), fill=part)
                        w0 = 2 * D if name == "v" else 3 * D
                        for j in range(2):
                            s = 2 * i + j
                            for kc in range(KC):
                                last = product(bk[:, j * D:(j + 1) * D], cols(AT, ALL, kc, slice(s * P, (s + 1) * P)),
                                               cols(WA, ALL, kc, slice(w0, w0 + D)), kc == 0, kc == KC - 1)
                        last.then_inc(filled, 1)
                    elif name in ("k", "q"):
                        w0 = (D if name == "k" else 0) + i * P
                        wait_drained(pe, a, ("turn", 0), ("turn", 1), fill=part)
                        for kc in range(KC):
                            last = product(bk[:, :], cols(WA, ALL, kc, slice(w0, w0 + P)),
                                           cols(AT, ALL, kc, ALL), kc == 0, kc == KC - 1)
                        last.then_inc(filled, 1)
                    elif name == "k_turn":
                        wait_drained(pe, a, ("k", i), fill=part)
                        for c in range(SUBS - 1):
                            last = nc.tensor.transpose(bk[:, c * P:(c + 1) * P], kf[:, i, c * P:(c + 1) * P], ident)
                        last.then_inc(filled, 1)
                    elif name == "state":
                        m, c = i // SUBS, i % SUBS
                        wait_drained(pe, a, ("k_turn", m), ("v", (c - 1) // 2), fill=part)
                        nc.tensor.matmul(bk[:, 0:MH * VW], k_tok[:, m, c - 1, :],
                                         v_aug[:, c - 1, m * MH:(m + 1) * MH, :].rearrange("p h d -> p (h d)"),
                                         start=True, stop=True).then_inc(filled, 1)
                    elif name == "scores":
                        m, c0, g = i // 8, 2 * (i // 4 % 2), i % 4
                        wait_drained(pe, a, fill=part)
                        pe.wait_ge(k_lo_done, 2 * a + m + 1)
                        pe.wait_ge(q_lo_done, 4 * a + 2 * m + 2)
                        rows = slice(32 * g, 32 * g + 32)
                        for j in range(2):
                            cs = slice((c0 + j) * P, (c0 + j + 1) * P)
                            last = product(bk[:, j * 2 * P:(j + 1) * 2 * P].rearrange("p (h q) -> p h q", h=2),
                                           (k_hi[rows, m, cs], k_lo[rows, m, cs]),
                                           (q_hi[rows, m, :, cs], q_lo[rows, m, :, cs]), True, True)
                        last.then_inc(filled, 1)
                    elif name == "values":
                        m = i // 2
                        wait(pe, heads_done, 4 * a + i)
                        for c in (2 * (i % 2), 2 * (i % 2) + 1):
                            r = c % 2
                            if c == 1:
                                wait_drained(pe, a, ("state", m * SUBS + 1))
                            elif c > 1:
                                pe.wait_ge(state_done, 4 * a + 2 * m + c - 1)
                            if c:
                                nc.tensor.matmul(o_bank[:, r, :], qf[:, m, c * P:(c + 1) * P], st[:, c % 2, :],
                                                 start=(r == 0), stop=False, skip_group_check=True)
                            for h in range(MH):
                                n = 4 * i + h // 2
                                if r == 0 and h % 2 == 0:
                                    wait_drained(pe, a, ("scores", n), ("v", c // 2))
                                last = nc.tensor.matmul(o_bank[:, r, h * VW:(h + 1) * VW],
                                                        scores[:, n % SM, 2 * r + h % 2, :],
                                                        v_aug[:, c, m * MH + h, :], start=(c == 0 and h == 0),
                                                        stop=True, skip_group_check=True)
                        last.then_inc(o_filled, 1)
                    elif name == "router":
                        wait_drained(pe, a, ("turn", 4), ("turn", 5), fill=part)
                        if isinstance(a, int) and a == 0:
                            pe.wait_ge(split_lo, NP + 1)
                        for s in range(SUBS):
                            ss = slice(s * P, (s + 1) * P)
                            dst = bk[:, s * 2 * E:(s + 1) * 2 * E]
                            for kc in range(KC):
                                nc.tensor.matmul(dst, XA[0][:, kc, ss],
                                                 wr_parts[:, kc, :, :].rearrange("p t e -> p (t e)"),
                                                 start=(s == 0 and kc == 0), stop=False, skip_group_check=True)
                                last = nc.tensor.matmul(dst[:, 0:E], XA[1][:, kc, ss], wr_parts[:, kc, 0, :],
                                                        start=False, stop=(kc == KC - 1), skip_group_check=True)
                        last.then_inc(filled, 1)
                    elif name == "weights_turn":
                        wait_drained(pe, a, fill=part)
                        pe.wait_ge(cw_ready, a + 1)
                        nc.tensor.transpose(bk[0:E * SUBS, 0:P], cw[:, :, :].rearrange("p e s -> p (e s)"), ident)\
                            .then_inc(filled, 1)

            run(step, pe)


CHAIN_A = 30
C_IDENT = 0
C_CAUSAL = C_IDENT + P
C_BLOCK = C_CAUSAL + P
C_EO = C_BLOCK + MH * VW
C_TIE_E = C_EO + 2
C_TIE_G = C_TIE_E + E * E
C_POW = C_TIE_G + GROUPS * GROUPS
CONST_COLS = C_POW + SUBS


def constants():
    c = np.zeros((P, CONST_COLS), np.float32)
    p = np.arange(P)
    c[:, C_IDENT:C_IDENT + P] = np.eye(P)
    c[:, C_CAUSAL:C_CAUSAL + P] = p[None, :] >= p[:, None]
    c[:, C_BLOCK:C_BLOCK + MH * VW] = (p[:, None] // DH) == (np.arange(MH * VW)[None, :] // VW)
    c[:, C_EO] = (p // DH) % 2 == 0
    c[:, C_EO + 1] = (p // DH) % 2 == 1
    for at, n in ((C_TIE_E, E), (C_TIE_G, GROUPS)):
        c[:, at:at + n * n] = (np.arange(n)[None, :] < np.arange(n)[:, None]).reshape(-1)
    c[:, C_POW:C_POW + SUBS] = -0.5
    return c


def kernel(**inputs):
    import concourse.bacc as bacc
    from concourse.bass_utils import run_bass_kernel_spmd

    g = {k.removeprefix("L0_"): np.asarray(v) for k, v in inputs.items()}
    qkvo = np.concatenate([g["attn_" + n].T for n in ("Wq", "Wk", "Wv", "Wo")], axis=1)
    gate = np.concatenate([g["ffn_Wg_s"][None], g["ffn_Wg"]])
    up = np.concatenate([g["ffn_Wu_s"][None], g["ffn_Wu"]])
    down = np.concatenate([g["ffn_Wd_s"][None], g["ffn_Wd"]])
    gu = np.stack([gate, up], axis=1).reshape(SLOTS, 2, KC, P, FF).transpose(3, 0, 1, 2, 4)
    arrays = {
        "x": g["attn_x"],
        "w_qkvo": qkvo.reshape(KC, P, 4 * D).transpose(1, 0, 2),
        "w_gate_up": gu.reshape(P, SLOTS * 2 * KC * FF),
        "w_down": down.transpose(1, 0, 2).reshape(P, SLOTS * D),
        "w_router": g["ffn_gate_w"].T.reshape(KC, P, E).transpose(1, 0, 2),
        "bias": g["ffn_correction_bias"],
        "consts": constants(),
    }
    nc = bacc.Bacc("TRN2", target_bir_lowering=False, num_devices=1)
    ins, args = {}, []
    for name, v in arrays.items():
        v = np.ascontiguousarray(v)
        ins[f"in_{name}"] = v
        args.append(nc.dram_tensor(f"in_{name}", v.shape, mybir.dt.from_np(v.dtype), kind="ExternalInput").ap())
    args.append(nc.dram_tensor("out_y", (B, S, D), mybir.dt.float32, kind="ExternalOutput").ap())
    linear_attention_moe(nc, *args)
    r = run_bass_kernel_spmd(nc, [ins], core_ids=[0])
    return r.results[0]["out_y"]
```

```python
import concourse.bass as bass
from concourse import mybir
from contextlib import ExitStack
import numpy as np

B, S, D = 16, 512, 256
H, DH = 16, 16
E, FF = 8, 128
GROUPS, TOP_GROUPS, TOP_K = 4, 2, 4
ROUTE_SCALE = 2.5
LN_EPS, ATT_EPS, ROUTE_EPS = 1e-5, 1e-8, 1e-20

P = 128
SUBS = S // P
KC = D // P
MH = P // DH
PAIRS = H // 2
PER_G = E // GROUPS
SLOTS = E + 1

ET, HR, CW, SM, GB = 3, 3, 4, 8, 3

def scores(j, g):
    return [("scores", 4 * j + g)]


def values(j, g):
    return [("values", 4 * j + g)]


def states(m):
    return [("state", m * SUBS + c) for c in range(1, SUBS)]


def scores_and_values(j, between):
    out = []
    for g in range(4):
        out += scores(j, g) + values(j - 1, g)
        out += between.get(g, [])
    return out


SCHEDULE = (
    [("gate", 0), ("up", 0), ("turn", 0), ("turn", 1), ("split", 0), ("gate", 1),
     ("k", 0), ("q", 0), ("up", 1), ("k", 1), ("q", 1), ("k_split", 0), ("q_split", 0), ("split", 1),
     ("down", 0), ("v", 0), ("v", 1), ("k_split", 1), ("q_split", 1), ("gate", 2),
     ("k_turn", 0), ("k_turn", 1), ("cum", 0), ("cum", 1), ("up", 2)]
    + states(0) + scores(0, 0) + scores(0, 1) + [("split", 2), ("down", 1)] + scores(0, 2) + scores(0, 3)
    + [("gate", 3)]
    + scores_and_values(1, {1: [("den_turn", 0)], 2: [("up", 3)], 3: [("den_turn", 1)]})
    + [("inter", 0), ("split", 3), ("down", 2)]
    + scores(2, 0) + scores(2, 1) + [("gate", 4)]
    + scores(2, 2) + values(1, 0) + values(1, 1) + scores(2, 3) + values(1, 2) + values(1, 3)
    + [("inter", 1), ("up", 4)] + states(1) + [("down", 3), ("split", 4)]
    + scores_and_values(3, {0: [("spread", 0)], 1: [("gate", 5)], 3: [("up", 5)]})
    + [("inter", 2), ("split", 5), ("down", 4)]
    + values(3, 0) + values(3, 1) + values(3, 2) + values(3, 3)
    + [("inter", 3), ("gate", 6), ("spread", 1), ("up", 6), ("split", 6), ("down", 5),
       ("wo", 0), ("wo", 1), ("ln2_stats", 0),
       ("gate", 7), ("up", 7), ("ln2_apply", 0), ("down", 6), ("split", 7),
       ("turn", 2), ("turn", 3), ("ln1_stats", 0), ("ln1_apply", 0), ("gate", 8), ("router", 0), ("up", 8),
       ("route", 0), ("down", 7), ("split", 8), ("down", 8), ("weights_turn", 0), ("result", 0)]
)
EXPERT_PARTS = ("gate", "up", "split", "down", "result")
FIRST_NORM = [("ln1_stats", 0), ("ln1_apply", 0)]
ATTENTION = [x for x in SCHEDULE if x[0] not in EXPERT_PARTS]
EXPERTS = [x for x in SCHEDULE if x[0] in EXPERT_PARTS]
BANKED = ("turn", "v", "k", "q", "k_turn", "state", "scores", "den_turn", "spread", "wo", "router",
          "weights_turn")
USE = {x: n for n, x in enumerate(x for x in SCHEDULE if x[0] in BANKED)}
USES = len(USE)
assert USES % 2 == 0


def linear_attention_moe(nc, x, w_qkvo, w_gate_up, w_down, w_router, bias, consts, out):
    f32, f32r = mybir.dt.float32, mybir.dt.float32r
    ALU, ACT, AX = mybir.AluOpType, mybir.ActivationFunctionType, mybir.AxisListType

    ctx = ExitStack()
    with ctx:
        def sb(name, shape, dt=f32):
            return ctx.enter_context(nc.sbuf_tensor(name, shape, dt))

        def ps(name, shape):
            return ctx.enter_context(nc.psum_tensor(name, shape, f32))

        def sem(name):
            return ctx.enter_context(nc.semaphore(name))

        wa_hi, wa_lo = (sb(f"wa_{n}", [P, KC, 4 * D], f32r) for n in ("hi", "lo"))
        wg_hi, wg_lo = (sb(f"wg_{n}", [P, SLOTS, 2, KC, FF], f32r) for n in ("hi", "lo"))
        wd_hi, wd_lo = (sb(f"wd_{n}", [P, SLOTS, D], f32r) for n in ("hi", "lo"))
        wr_parts = sb("wr_parts", [P, KC, 2, E], f32r)
        wr_raw = sb("wr_raw", [P, KC, E])
        bias_sb = sb("bias_sb", [P, E])
        cst = sb("cst", [P, CONST_COLS])
        ident = cst[:, C_IDENT:C_IDENT + P]
        causal = cst[:, C_CAUSAL:C_CAUSAL + P]
        block_mask = cst[:, C_BLOCK:C_BLOCK + P]
        one = cst[:, C_ONE:C_ONE + 1]
        before_e = cst[:, C_TIE_E:C_TIE_E + E * E].rearrange("p (a b) -> p a b", a=E)
        before_g = cst[:, C_TIE_G:C_TIE_G + GROUPS * GROUPS].rearrange("p (a b) -> p a b", a=GROUPS)
        power = cst[:, C_POW:C_POW + SUBS]

        x_in = sb("x_in", [P, SUBS, D])
        x_mid = [sb(f"x_mid{i}", [P, SUBS, D]) for i in range(2)]
        norm1 = sb("norm1", [P, SUBS, D])
        at_hi, at_lo = (sb(f"at_{n}", [P, KC, S], f32r) for n in ("hi", "lo"))
        num_t = sb("num_t", [P, KC, S])
        norm2 = num_t[:, :, :].rearrange("p k (a d) -> p (k a) d", d=D)
        xt_hi, xt_lo = ([sb(f"xt_{n}{i}", [P, KC, S], f32r) for i in range(2)] for n in ("hi", "lo"))
        kf, qf = sb("kf", [P, KC, S]), sb("qf", [P, KC, S])
        expo = sb("expo", [P, 2, S])
        k_hi, k_lo = (sb(f"k_{n}", [P, KC, S], f32r) for n in ("hi", "lo"))
        q_hi, q_lo = (sb(f"q_{n}", [P, KC, 2, S], f32r) for n in ("hi", "lo"))
        k_tok = sb("k_tok", [P, KC, SUBS - 1, P])
        v_win = sb("v_win", [P, SUBS, PAIRS, 3, DH])
        scores = sb("scores", [P, SM, 4, P])
        st = sb("st", [P, SUBS - 1, P])
        st_new = sb("st_new", [P, P])
        den = sb("den", [P, SUBS, MH])
        rden = sb("rden", [P, KC, SUBS, MH])
        stats = sb("stats", [P, SUBS, 6])
        m_sum, m_dif, v_sum, mean = (sb(n, [P, SUBS]) for n in ("m_sum", "m_dif", "v_sum", "mean"))
        veps = sb("veps", [P, SUBS])
        rstd = sb("rstd", [P, SUBS])
        spare = num_t[:, :, :].rearrange("p k n -> p (k n)")

        def compared(at, n):
            c, q = at + SUBS * n * 2 * n, SUBS * n * n
            return (spare[:, at:c].rearrange("p (s a t b) -> p s a t b", s=SUBS, a=n, t=2),
                    spare[:, c:c + q].rearrange("p (s a b) -> p s a b", s=SUBS, a=n))

        e_cmp, e_eq = compared(0, E)
        g_cmp, g_eq = compared(3 * SUBS * E * E, GROUPS)
        logit = sb("logit", [P, SUBS, E])
        sig = sb("sig", [P, SUBS, E])
        sig_c = sb("sig_c", [P, SUBS, E])
        g_sum = sb("g_sum", [P, SUBS, GROUPS])
        g_rank = sb("g_rank", [P, SUBS, GROUPS])
        choice = sb("choice", [P, SUBS, E])
        e_rank = sb("e_rank", [P, SUBS, E])
        w_sel = sb("w_sel", [P, SUBS, E])
        w_sum = sb("w_sum", [P, SUBS])
        w_rec = sb("w_rec", [P, SUBS])
        cw = sb("cw", [P, E, SUBS])
        cw_t = sb("cw_t", [E * SUBS, P])
        cw_all = sb("cw_all", [P, CW, S])
        stage = cw_all[:, :, :].rearrange("p (a s) n -> p a (s n)", a=2)
        et = sb("et", [P, ET, S])
        h_hi, h_lo = (sb(f"h_{n}", [P, HR, S], f32r) for n in ("hi", "lo"))

        bank = [ps(f"bank{i}", [P, S]) for i in range(2)]
        o_bank = ps("o_bank", [P, S])
        g_bank = [ps(f"g_bank{i}", [P, S]) for i in range(GB)]
        y_bank = [ps(f"y_bank{i}", [P, 2, D]) for i in range(2)]
        cw_dram = nc.dram_tensor("cw_dram", [2, E, S], f32, kind="Internal").ap()

        x_v = x.rearrange("b (s p) d -> b p s d", p=P)
        out_v = out.rearrange("b (s p) d -> b p s d", p=P)

        staged = [sem(f"staged{i}") for i in range(2)]
        small_in = sem("small_in")
        split_hi = sem("split_hi")
        split_lo = sem("split_lo")
        zeros_set = sem("zeros_set")
        x_loaded = sem("x_loaded")
        filled = sem("filled")
        drained = [sem(f"drained{i}") for i in range(2)]
        turn_hi = sem("turn_hi")
        exp_done = sem("exp_done")
        relu_done = sem("relu_done")
        k_hi_done, k_lo_done = sem("k_hi_done"), sem("k_lo_done")
        q_hi_done, q_lo_done = sem("q_hi_done"), sem("q_lo_done")
        state_done = sem("state_done")
        values_done = sem("values_done")
        o_filled = sem("o_filled")
        num_done = sem("num_done")
        cum_done = sem("cum_done")
        qk_done = sem("qk_done")
        rden_done = sem("rden_done")
        rden_wide = sem("rden_wide")
        att_hi_done, att_lo_done = sem("att_hi_done"), sem("att_lo_done")
        var_ready, rstd_ready = sem("var_ready"), sem("rstd_ready")
        norm_ready = sem("norm_ready")
        expn_done = sem("expn_done")
        cw_ready = sem("cw_ready")
        cw_stored = sem("cw_stored")
        cw_loaded = [sem(f"cw_loaded{i}") for i in range(CW)]
        cw_used = sem("cw_used")
        g_filled = sem("g_filled")
        g_drained = sem("g_drained")
        tanh_done = sem("tanh_done")
        h_hi_done, h_lo_done = sem("h_hi_done"), sem("h_lo_done")
        down_done = sem("down_done")
        y_drained = sem("y_drained")
        out_sent = [sem(f"out_sent{i}") for i in range(2)]
        chain_a, chain_e = sem("chain_a"), sem("chain_e")

        def wait(eng, s, value):
            if isinstance(value, int) and value <= 0:
                return
            eng.wait_ge(s, value)

        def wait_filled(eng, b, part):
            eng.wait_ge(filled, USES * b + USE[part] + 1)

        def wait_drained(eng, b, *parts, fill=None):
            need = [0, 0]
            for part in parts:
                n = USE[part]
                need[n % 2] = max(need[n % 2], n // 2 + 1)
            if fill:
                n = USE[fill]
                need[n % 2] = max(need[n % 2], n // 2)
            for j in range(2):
                if need[j] or (fill and USE[fill] % 2 == j):
                    wait(eng, drained[j], USES // 2 * b + need[j])

        def bank_of(part):
            return bank[USE[part] % 2]

        def run(step, eng):
            step(FIRST_NORM, -2, -1, 0)
            step(ATTENTION, -1, -1, 1)
            step(SCHEDULE, 0, 0, 0)
            with eng.Fori(0, (B - 2) // 2) as k:
                step(SCHEDULE, k * 2 + 1, k, 1)
                step(SCHEDULE, k * 2 + 2, k + 1, 0)
            step(EXPERTS, B - 1, (B - 1) // 2, 1)

        PIECES = []
        for kc in range(KC):
            PIECES.append((w_qkvo[:, kc], 4 * D, wa_hi[:, kc], wa_lo[:, kc]))
        GU = 2 * KC * FF
        for s in range(0, SLOTS, 2):
            n = min(2, SLOTS - s)
            PIECES.append((w_gate_up[:, s * GU:(s + n) * GU], n * GU,
                           wg_hi[:, s:s + n].rearrange("p s g k f -> p (s g k f)"),
                           wg_lo[:, s:s + n].rearrange("p s g k f -> p (s g k f)")))
        for s in range(0, SLOTS, 4):
            n = min(4, SLOTS - s)
            PIECES.append((w_down[:, s * D:(s + n) * D], n * D,
                           wd_hi[:, s:s + n].rearrange("p s n -> p (s n)"),
                           wd_lo[:, s:s + n].rearrange("p s n -> p (s n)")))
        NP = len(PIECES)
        SPLIT_EVERY = 4

        def piece_after(parts, t):
            n = KC + t // SPLIT_EVERY
            return n if parts is ATTENTION and t % SPLIT_EVERY == 0 and n <= NP else None

        block = ctx.enter_context(nc.Block())

        @block.sync
        def _(sp):
            def load_x(b):
                sp.dma_start(x_in[:, :, :], x_v[b] if isinstance(b, int) else
                             x_v[bass.ds(b, 1)].rearrange("a p s d -> p (a s) d")).then_inc(x_loaded, 16)

            load_x(0)
            sp.dma_start(cst[:, :], consts).then_inc(small_in, 16)
            sp.dma_start(bias_sb[:, :], bias.partition_broadcast(P)).then_inc(small_in, 16)
            sp.dma_start(wr_raw[:, :, :], w_router).then_inc(small_in, 16)
            for n, (src, cols, _, _) in enumerate(PIECES):
                if n >= 2:
                    sp.wait_ge(split_lo, n - 1)
                sp.dma_start(stage[:, n % 2, 0:cols], src).then_inc(staged[n % 2], 16)

            def step(parts, b, half, parity):
                a, pa = b + 1, 1 - parity
                if parts is EXPERTS or parts is SCHEDULE:
                    if isinstance(b, int) and b == 0:
                        sp.wait_ge(split_lo, NP)
                    for e in range(CW):
                        load_cw(b, parity, e)
                for name, i in parts:
                    if name == "down" and i < E - CW:
                        load_cw(b, parity, i + CW)
                    elif name == "ln2_stats":
                        wait_drained(sp, a, ("wo", 1))
                        next_x(a)
                    elif name == "weights_turn":
                        wait_drained(sp, a, ("weights_turn", 0))
                        sp.dma_start(cw_dram[pa].rearrange("e (s p) -> (e s) p", p=P), cw_t[:, :])\
                            .then_inc(cw_stored, 16)
                    elif name == "result":
                        sp.wait_ge(y_drained, 2 * b + 2)
                        sp.dma_start(out_v[b] if isinstance(b, int) else
                                     out_v[bass.ds(b, 1)].rearrange("a p s d -> p (a s) d"),
                                     x_mid[parity][:, :, :]).then_inc(out_sent[parity], 16)

            def next_x(a):
                load_x((a + 1) % B)

            def load_cw(b, parity, e):
                if e == 0:
                    sp.wait_ge(cw_stored, 16 * b + 16)
                wait(sp, cw_used, E * b + e - CW + 1)
                sp.dma_start(cw_all[:, e % CW, :], cw_dram[parity, e].partition_broadcast(P))\
                    .then_inc(cw_loaded[e % CW], 16)

            run(step, sp)
            sp.wait_ge(out_sent[0], 16 * (B // 2))
            sp.wait_ge(out_sent[1], 16 * (B // 2))
            sp.wait_ge(x_loaded, 16 * (B + 1))

        @block.scalar
        def _(act):
            def weights_high(n):
                if n < NP:
                    _, cols, hi, _ = PIECES[n]
                    act.wait_ge(staged[n % 2], 16 * (n // 2 + 1))
                    nc.scalar.activation(hi, stage[:, n % 2, 0:cols], ACT.Copy).then_inc(split_hi, 1)
                else:
                    nc.scalar.activation(wr_parts[:, :, 0, :], wr_raw[:, :, :], ACT.Copy).then_inc(split_hi, 1)

            act.wait_ge(small_in, 48)
            for n in range(KC):
                weights_high(n)

            def step(parts, b, half, parity):
                a, pa = b + 1, 1 - parity

                def h_high(e):
                    if e == 0:
                        act.wait_ge(g_drained, 2 * SLOTS * b + 2)
                    else:
                        act.wait_ge(cw_used, E * b + e)
                    wait(act, down_done, SLOTS * b + e - HR + 1)
                    nc.scalar.activation(h_hi[:, e % HR, :], et[:, e % ET, :], ACT.Copy)\
                        .then_inc(h_hi_done, 1)

                for t, (name, i) in enumerate(parts):
                    part = (name, i)
                    if piece_after(parts, t) is not None:
                        weights_high(piece_after(parts, t))
                    if name == "gate":
                        act.wait_ge(g_filled, 2 * SLOTS * b + 2 * i + 1)
                        wait(act, h_lo_done, SLOTS * b + i - ET + 1)
                        nc.scalar.activation(et[:, i % ET, :], g_bank[2 * i % GB][:, :], ACT.Tanh,
                                             scale=0.5).then_inc(tanh_done, 1)
                    elif name == "split":
                        h_high(i)
                    elif name == "turn":
                        wait_filled(act, a, part)
                        dst = at_hi if i < 2 else xt_hi[pa]
                        nc.scalar.activation(dst[:, i % 2, :], bank_of(part)[:, :], ACT.Copy)\
                            .then_inc(turn_hi, 1)
                    elif name == "v":
                        if i == 0:
                            act.wait_ge(zeros_set, 1)
                        wait_filled(act, a, part)
                        nc.scalar.activation(v_win[:, 2 * i:2 * i + 2, :, 0:3:2, :]
                                             .rearrange("p s g t d -> p (s g) t d"),
                                             bank_of(part)[:, :].rearrange("p (g t d) -> p g t d", t=2, d=DH),
                                             ACT.Copy).then_inc(drained[USE[part] % 2], 1)
                    elif name in ("k", "q"):
                        n = 2 * i + (name == "q")
                        wait_filled(act, a, part)
                        if i > 0:
                            wait_drained(act, a, (name, i - 1))
                        nc.scalar.activation(expo[:, n % 2, :], bank_of(part)[:, :], ACT.Relu, scale=-1.0)\
                            .then_inc(relu_done, 1)
                        act.wait_ge(relu_done, 4 * a + n + 1)
                        nc.scalar.activation(expo[:, n % 2, :], expo[:, n % 2, :], ACT.Exp, scale=-1.0)\
                            .then_inc(exp_done, 1)
                    elif name == "k_split":
                        wait_drained(act, a, ("k", i))
                        nc.scalar.activation(k_hi[:, i, :], kf[:, i, :], ACT.Copy).then_inc(k_hi_done, 1)
                    elif name == "q_split":
                        wait_drained(act, a, ("q", i))
                        for j in range(2):
                            nc.scalar.activation(q_hi[:, i, j, :], qf[:, i, :], ACT.Copy,
                                                 scale=cst[:, C_EO + j:C_EO + j + 1]).then_inc(q_hi_done, 1)
                    elif name == "k_turn":
                        wait_filled(act, a, part)
                        nc.scalar.activation(k_tok[:, i, :, :].rearrange("p c d -> p (c d)"),
                                             bank_of(part)[:, 0:(SUBS - 1) * P], ACT.Copy)\
                            .then_inc(drained[USE[part] % 2], 1)
                    elif name == "den_turn":
                        act.wait_ge(rden_done, 2 * a + i + 1)
                        nc.scalar.activation(expo[:, i, :].rearrange("p (a d) -> p a d", d=DH),
                                             rden[:, i, :, :].rearrange("p s h -> p (s h)").unsqueeze(2)
                                             .broadcast_to([P, S // DH, DH]), ACT.Copy).then_inc(rden_wide, 1)
                    elif name == "inter" and i % 2 == 1:
                        act.wait_ge(o_filled, 2 * a + i // 2 + 1)
                        nc.scalar.activation(num_t[:, i // 2, :], o_bank[:, :], ACT.Copy).then_inc(num_done, 1)
                    elif name == "spread":
                        wait_drained(act, a, part)
                        nc.scalar.activation(at_hi[:, i, :], num_t[:, i, :], ACT.Copy).then_inc(att_hi_done, 1)
                    elif name == "route":
                        wait_drained(act, a, ("router", 0))
                        nc.scalar.activation(sig[:, :, :], logit[:, :, :], ACT.Exp, scale=-1.0)\
                            .then_inc(expn_done, 1)
                    elif name == "weights_turn":
                        wait_filled(act, a, part)
                        wait(act, cw_stored, 16 * a)
                        nc.scalar.activation(cw_t[:, :], bank_of(part)[0:E * SUBS, 0:P], ACT.Copy)\
                            .then_inc(drained[USE[part] % 2], 1)

            run(step, act)

        @block.gpsimd
        def _(pool):
            nc.gpsimd.memset(v_win[:, :, :, 1, :], 0.0).then_inc(zeros_set, 1)
            pool.wait_ge(small_in, 48)

            def step(parts, b, half, parity):
                a = b + 1

                def weigh(e):
                    if e == 0:
                        return
                    r = (e - 1) % CW
                    pool.wait_ge(cw_loaded[r], 16 * (E // CW * b + (e - 1) // CW + 1))
                    pool.wait_ge(g_drained, 2 * SLOTS * b + 2 * e + 2)
                    nc.gpsimd.tensor_tensor(et[:, e % ET, :], et[:, e % ET, :], cw_all[:, r, :], ALU.mult)\
                        .then_inc(cw_used, 1)

                def h_low(e):
                    pool.wait_ge(h_hi_done, SLOTS * b + e + 1)
                    nc.gpsimd.tensor_tensor(h_lo[:, e % HR, :], et[:, e % ET, :],
                                            h_hi[:, e % HR, :].bitcast(f32), ALU.subtract)\
                        .then_inc(h_lo_done, 1)

                for name, i in parts:
                    if name == "up":
                        weigh(i)
                    elif name == "split":
                        h_low(i)
                    elif name == "cum":
                        pool.wait_ge(cum_done, 2 * a + i + 1)
                        nc.gpsimd.tensor_tensor(expo[:, i, :], expo[:, i, :], qf[:, i, :], ALU.mult)\
                            .then_inc(qk_done, 1)
                    elif name in ("ln1_apply", "ln2_apply"):
                        pool.wait_ge(var_ready, 2 * a + (3 if name == "ln1_apply" else 2))
                        nc.gpsimd.tensor_tensor(rstd[:, :], veps[:, :], power, ALU.pow)\
                            .then_inc(rstd_ready, 1)

            run(step, pool)

        @block.vector
        def _(dve):
            dve.wait_ge(small_in, 48)

            def weights_low(n):
                dve.wait_ge(split_hi, n + 1)
                if n < NP:
                    _, cols, hi, lo = PIECES[n]
                    nc.vector.tensor_tensor(lo, stage[:, n % 2, 0:cols], hi.bitcast(f32), ALU.subtract)\
                        .then_inc(split_lo, 1)
                else:
                    nc.vector.tensor_tensor(wr_parts[:, :, 1, :], wr_raw[:, :, :],
                                            wr_parts[:, :, 0, :].bitcast(f32), ALU.subtract).then_inc(split_lo, 1)

            def step(parts, b, half, parity):
                a, pa = b + 1, 1 - parity
                own = [0 if parts is FIRST_NORM else CHAIN_A * a + CHAIN_NORM]

                def link(ins):
                    own[0] += 1
                    ins.then_inc(chain_a, 1)
                    dve.wait_ge(chain_a, own[0])

                def layernorm_stats(src, n):
                    wait(dve, norm_ready, n - 1)
                    for s in range(SUBS):
                        last = nc.vector.bn_stats(stats[:, s, :], src[:, s, :])
                    link(last)
                    m0, m1, v0, v1 = (stats[:, :, j] for j in (1, 4, 2, 5))
                    nc.vector.tensor_tensor(m_sum[:, :], m0, m1, ALU.add)
                    nc.vector.tensor_tensor(m_dif[:, :], m0, m1, ALU.subtract)
                    link(nc.vector.tensor_tensor(v_sum[:, :], v0, v1, ALU.add))
                    nc.vector.tensor_scalar(mean[:, :], m_sum[:, :], 0.5, None, ALU.mult)
                    nc.vector.scalar_tensor_tensor(m_dif[:, :], m_dif[:, :], 0.25, m_dif[:, :],
                                                   ALU.mult, ALU.mult)
                    link(nc.vector.tensor_scalar(v_sum[:, :], v_sum[:, :], 1.0 / D, LN_EPS, ALU.mult, ALU.add))
                    nc.vector.tensor_tensor(veps[:, :], m_dif[:, :], v_sum[:, :], ALU.add)\
                        .then_inc(var_ready, 1)

                def layernorm_apply(src, norm, n):
                    dve.wait_ge(rstd_ready, n)
                    for s in range(SUBS):
                        last = nc.vector.tensor_scalar(norm[:, s, :], src[:, s, :], mean[:, s:s + 1],
                                                       rstd[:, s:s + 1], ALU.subtract, ALU.mult)
                    last.then_inc(norm_ready, 1)

                def beaten(values, n, cmp, eq, before, rank):
                    other = values.unsqueeze(2).broadcast_to([P, SUBS, n, n])
                    own_v = values.unsqueeze(3).broadcast_to([P, SUBS, n, n])
                    nc.vector.tensor_tensor(cmp[:, :, :, 0, :], other, own_v, ALU.is_gt)
                    link(nc.vector.tensor_tensor(eq[:, :, :, :], other, own_v, ALU.is_equal))
                    link(nc.vector.tensor_tensor(cmp[:, :, :, 1, :], eq[:, :, :, :],
                                                 before.unsqueeze(1).broadcast_to([P, SUBS, n, n]),
                                                 ALU.mult))
                    link(nc.vector.tensor_reduce(rank[:, :, :],
                                                 cmp[:, :, :, :, :].rearrange("p s a t b -> p (s a) (t b)"),
                                                 AX.X, ALU.add))

                if parts is ATTENTION:
                    for n in range(KC):
                        weights_low(n)
                for t, (name, i) in enumerate(parts):
                    part = (name, i)
                    if piece_after(parts, t) is not None:
                        weights_low(piece_after(parts, t))
                    if name == "gate":
                        dve.wait_ge(tanh_done, SLOTS * b + i + 1)
                        nc.vector.scalar_tensor_tensor(et[:, i % ET, :], et[:, i % ET, :], 1.0,
                                                       g_bank[2 * i % GB][:, :], ALU.add, ALU.mult)\
                            .then_inc(g_drained, 1)
                    elif name == "up":
                        dve.wait_ge(g_filled, 2 * SLOTS * b + 2 * i + 2)
                        dve.wait_ge(g_drained, 2 * SLOTS * b + 2 * i + 1)
                        nc.vector.scalar_tensor_tensor(et[:, i % ET, :], et[:, i % ET, :], 0.5,
                                                       g_bank[(2 * i + 1) % GB][:, :], ALU.mult, ALU.mult)\
                            .then_inc(g_drained, 1)
                    elif name == "result":
                        dve.wait_ge(down_done, SLOTS * b + SLOTS)
                        for j in range(2):
                            xm = x_mid[parity][:, 2 * j:2 * j + 2, :]
                            nc.vector.tensor_tensor(xm, xm, y_bank[j][:, :, :], ALU.add)\
                                .then_inc(y_drained, 1)
                    elif name == "ln1_stats":
                        dve.wait_ge(x_loaded, 16 * a + 32)
                        layernorm_stats(x_in, 2 * a + 3)
                    elif name == "ln1_apply":
                        layernorm_apply(x_in, norm1, 2 * a + 3)
                    elif name == "ln2_stats":
                        wait_drained(dve, a, ("wo", 0), ("wo", 1))
                        layernorm_stats(x_mid[pa], 2 * a + 2)
                    elif name == "ln2_apply":
                        layernorm_apply(x_mid[pa], norm2, 2 * a + 2)
                    elif name == "turn":
                        dve.wait_ge(turn_hi, 4 * a + i + 1)
                        dst, hi = (at_lo, at_hi) if i < 2 else (xt_lo[pa], xt_hi[pa])
                        nc.vector.tensor_tensor(dst[:, i % 2, :], bank_of(part)[:, :],
                                                hi[:, i % 2, :].bitcast(f32), ALU.subtract)\
                            .then_inc(drained[USE[part] % 2], 1)
                    elif name in ("k", "q"):
                        n = 2 * i + (name == "q")
                        dve.wait_ge(exp_done, 4 * a + n + 1)
                        dst = kf if name == "k" else qf
                        nc.vector.scalar_tensor_tensor(dst[:, i, :], bank_of(part)[:, :], 0.0,
                                                       expo[:, n % 2, :], ALU.max, ALU.add)\
                            .then_inc(drained[USE[part] % 2], 1)
                    elif name == "k_split":
                        dve.wait_ge(k_hi_done, 2 * a + i + 1)
                        nc.vector.tensor_tensor(k_lo[:, i, :], kf[:, i, :], k_hi[:, i, :].bitcast(f32),
                                                ALU.subtract).then_inc(k_lo_done, 1)
                    elif name == "q_split":
                        for j in range(2):
                            dve.wait_ge(q_hi_done, 4 * a + 2 * i + j + 1)
                            nc.vector.scalar_tensor_tensor(q_lo[:, i, j, :], qf[:, i, :],
                                                           cst[:, C_EO + j:C_EO + j + 1],
                                                           q_hi[:, i, j, :].bitcast(f32),
                                                           ALU.mult, ALU.subtract).then_inc(q_lo_done, 1)
                    elif name == "state":
                        c = i % SUBS
                        wait_filled(dve, a, part)
                        dst = st[:, 0, :] if c == 1 else st_new[:, :]
                        if c > 1:
                            wait(dve, state_done, 4 * a + 2 * (i // SUBS) + c - 2)
                        nc.vector.tensor_tensor(dst, bank_of(part)[:, 0:P], block_mask, ALU.mult)\
                            .then_inc(drained[USE[part] % 2], 1)
                        if c > 1:
                            wait_drained(dve, a, part)
                            nc.vector.tensor_tensor(st[:, c - 1, :], st[:, c - 2, :], st_new[:, :],
                                                    ALU.add).then_inc(state_done, 1)
                    elif name == "cum":
                        wait_drained(dve, a, ("k", 1), ("q", 1))
                        nc.vector.tensor_tensor_scan(expo[:, i, :], one.broadcast_to([P, S]), kf[:, i, :], 0.0,
                                                     ALU.mult, ALU.add).then_inc(cum_done, 1)
                    elif name == "scores":
                        wait_filled(dve, a, part)
                        wait(dve, values_done, 16 * a + i - SM + 1)
                        nc.vector.tensor_tensor(scores[:, i % SM, :, :],
                                                bank_of(part)[:, :].rearrange("p (h q) -> p h q", h=4),
                                                causal.unsqueeze(1).broadcast_to([P, 4, P]), ALU.mult)\
                            .then_inc(drained[USE[part] % 2], 1)
                    elif name == "den_turn":
                        wait_filled(dve, a, part)
                        nc.vector.tensor_reduce(den[:, :, :].rearrange("p s h -> p (s h)"),
                                                bank_of(part)[:, :].rearrange("p (a d) -> p a d", d=DH),
                                                AX.X, ALU.add).then_inc(drained[USE[part] % 2], 1)
                        wait_drained(dve, a, part)
                        link(nc.vector.tensor_scalar(den[:, :, :], den[:, :, :], ATT_EPS, None, ALU.add))
                        nc.vector.reciprocal(rden[:, i, :, :], den[:, :, :]).then_inc(rden_done, 1)
                        dve.wait_ge(rden_done, 2 * a + i + 1)
                    elif name == "spread":
                        wait_filled(dve, a, part)
                        dve.wait_ge(num_done, 2 * a + i + 1)
                        nc.vector.tensor_tensor(num_t[:, i, :], num_t[:, i, :], bank_of(part)[:, :], ALU.mult)\
                            .then_inc(drained[USE[part] % 2], 1)
                        dve.wait_ge(att_hi_done, 2 * a + i + 1)
                        nc.vector.tensor_tensor(at_lo[:, i, :], num_t[:, i, :], at_hi[:, i, :].bitcast(f32),
                                                ALU.subtract).then_inc(att_lo_done, 1)
                    elif name == "wo":
                        wait_filled(dve, a, part)
                        if i == 0:
                            wait(dve, out_sent[pa], 16 * half_of(b, half, parity))
                        nc.vector.tensor_tensor(x_mid[pa][:, 2 * i:2 * i + 2, :],
                                                bank_of(part)[:, :].rearrange("p (s d) -> p s d", s=2),
                                                x_in[:, 2 * i:2 * i + 2, :], ALU.add)\
                            .then_inc(drained[USE[part] % 2], 1)
                    elif name == "router":
                        wait_filled(dve, a, part)
                        nc.vector.tensor_reduce(
                            logit[:, :, :].rearrange("p s e -> p (s e)"),
                            bank_of(part)[:, 0:SUBS * 2 * E].rearrange("p (s t e) -> p s e t", s=SUBS, t=2),
                            AX.X, ALU.add).then_inc(drained[USE[part] % 2], 1)
                    elif name == "route":
                        dve.wait_ge(expn_done, a + 1)
                        link(nc.vector.tensor_scalar(sig_c[:, :, :], sig[:, :, :], 1.0, None, ALU.add))
                        link(nc.vector.reciprocal(sig[:, :, :], sig_c[:, :, :]))
                        link(nc.vector.tensor_tensor(sig_c[:, :, :], sig[:, :, :],
                                                     bias_sb[:, :].unsqueeze(1).broadcast_to([P, SUBS, E]), ALU.add))
                        pair = sig_c[:, :, :].rearrange("p s (g t) -> p s g t", t=PER_G)
                        link(nc.vector.tensor_tensor(g_sum[:, :, :], pair[:, :, :, 0], pair[:, :, :, 1], ALU.add))
                        beaten(g_sum[:, :, :], GROUPS, g_cmp, g_eq, before_g, g_rank)
                        link(nc.vector.tensor_scalar(g_rank[:, :, :], g_rank[:, :, :], TOP_GROUPS - 0.5, None,
                                                     ALU.is_lt))
                        link(nc.vector.tensor_tensor(choice[:, :, :].rearrange("p s (g t) -> p s g t", t=PER_G), pair,
                                                     g_rank[:, :, :].unsqueeze(3)
                                                     .broadcast_to([P, SUBS, GROUPS, PER_G]), ALU.mult))
                        beaten(choice[:, :, :], E, e_cmp, e_eq, before_e, e_rank)
                        link(nc.vector.scalar_tensor_tensor(w_sel[:, :, :], e_rank[:, :, :], TOP_K - 0.5,
                                                            sig[:, :, :], ALU.is_lt, ALU.mult))
                        link(nc.vector.tensor_reduce(w_sum[:, :], w_sel[:, :, :], AX.X, ALU.add))
                        link(nc.vector.tensor_scalar(w_sum[:, :], w_sum[:, :], ROUTE_EPS, None, ALU.add))
                        link(nc.vector.reciprocal(w_rec[:, :], w_sum[:, :]))
                        nc.vector.scalar_tensor_tensor(cw[:, :, :].rearrange("p e s -> p s e"), w_sel[:, :, :],
                                                       ROUTE_SCALE,
                                                       w_rec[:, :].unsqueeze(2).broadcast_to([P, SUBS, E]),
                                                       ALU.mult, ALU.mult).then_inc(cw_ready, 1)

                if isinstance(a, int) and "route" in dict(parts):
                    assert own[0] == CHAIN_A * (a + 1) + CHAIN_NORM

            def half_of(b, half, parity):
                return half + 1 if parity == 1 else half

            run(step, dve)

        @block.tensor
        def _(pe):
            def product(dst, lhs, rhs, first, last, shared=False):
                (lh, ll), (rh, rl) = lhs, rhs
                for n, (l, r) in enumerate(((lh, rh), (lh, rl), (ll, rh))):
                    ins = nc.tensor.matmul(dst, l, r, start=first and n == 0, stop=last and n == 2,
                                           skip_group_check=shared)
                return ins

            def cols(parts, *index):
                return tuple(p[index] for p in parts)

            WA, WG, WD = (wa_hi, wa_lo), (wg_hi, wg_lo), (wd_hi, wd_lo)
            AT = (at_hi, at_lo)
            ALL = slice(None)

            def step(parts, b, half, parity):
                a, pa = b + 1, 1 - parity
                XT, XA = (xt_hi[parity], xt_lo[parity]), (xt_hi[pa], xt_lo[pa])
                for name, i in parts:
                    part = (name, i)
                    if name in BANKED:
                        bk = bank_of(part)
                    if name in ("gate", "up"):
                        n = 2 * i + (name == "up")
                        if i == 0 and name == "gate":
                            wait_drained(pe, b, ("turn", 3))
                        wait(pe, g_drained, 2 * SLOTS * b + n - GB + 1)
                        if isinstance(b, int) and b == 0:
                            pe.wait_ge(split_lo, KC + i // 2 + 1)
                        for kc in range(KC):
                            last = product(g_bank[n % GB][:, :], cols(WG, ALL, i, n % 2, kc, ALL),
                                           cols(XT, ALL, kc, ALL), kc == 0, kc == KC - 1)
                        last.then_inc(g_filled, 1)
                    elif name == "down":
                        pe.wait_ge(h_lo_done, SLOTS * b + i + 1)
                        if i == 0:
                            wait(pe, y_drained, 2 * b)
                        if isinstance(b, int) and b == 0:
                            pe.wait_ge(split_lo, KC + (SLOTS + 1) // 2 + i // 4 + 1)
                        for s in range(SUBS):
                            last = product(y_bank[s // 2][:, s % 2, :],
                                           (h_hi[:, i % HR, s * P:(s + 1) * P], h_lo[:, i % HR, s * P:(s + 1) * P]),
                                           cols(WD, ALL, i, ALL), i == 0 and s % 2 == 0, i == SLOTS - 1, shared=True)
                        last.then_inc(down_done, 1)
                    elif name == "turn":
                        norm = norm1 if i < 2 else norm2
                        if isinstance(a, int) and a == 0 and i == 0:
                            pe.wait_ge(small_in, 48)
                        if i % 2 == 0:
                            pe.wait_ge(norm_ready, 2 * a + i // 2 + 1)
                        wait_drained(pe, a, fill=part)
                        for s in range(SUBS):
                            last = nc.tensor.transpose(bk[:, s * P:(s + 1) * P],
                                                       norm[:, s, (i % 2) * P:(i % 2 + 1) * P], ident)
                        last.then_inc(filled, 1)
                    elif name in ("v", "wo"):
                        if name == "v":
                            wait_drained(pe, a, ("turn", 0), ("turn", 1), fill=part)
                            if isinstance(a, int) and a == 0:
                                pe.wait_ge(split_lo, KC)
                        else:
                            wait_drained(pe, a, fill=part)
                            pe.wait_ge(att_lo_done, 2 * a + 2)
                        w0 = 2 * D if name == "v" else 3 * D
                        for j in range(2):
                            s = 2 * i + j
                            for kc in range(KC):
                                last = product(bk[:, j * D:(j + 1) * D], cols(AT, ALL, kc, slice(s * P, (s + 1) * P)),
                                               cols(WA, ALL, kc, slice(w0, w0 + D)), kc == 0, kc == KC - 1)
                        last.then_inc(filled, 1)
                    elif name in ("k", "q"):
                        w0 = (D if name == "k" else 0) + i * P
                        wait_drained(pe, a, ("turn", 0), ("turn", 1), fill=part)
                        for kc in range(KC):
                            last = product(bk[:, :], cols(WA, ALL, kc, slice(w0, w0 + P)),
                                           cols(AT, ALL, kc, ALL), kc == 0, kc == KC - 1)
                        last.then_inc(filled, 1)
                    elif name == "k_turn":
                        wait_drained(pe, a, ("k", i), fill=part)
                        for c in range(SUBS - 1):
                            last = nc.tensor.transpose(bk[:, c * P:(c + 1) * P], kf[:, i, c * P:(c + 1) * P], ident)
                        last.then_inc(filled, 1)
                    elif name == "state":
                        m, c = i // SUBS, i % SUBS
                        wait_drained(pe, a, ("k_turn", m), ("v", (c - 1) // 2), fill=part)
                        nc.tensor.matmul(bk[:, 0:P].rearrange("p (g t d) -> p g t d", t=2, d=DH),
                                         k_tok[:, m, c - 1, :], v_win[:, c - 1, m * 4:(m + 1) * 4, 0:3:2, :],
                                         start=True, stop=True).then_inc(filled, 1)
                    elif name == "scores":
                        m, c0, g = i // 8, 2 * (i // 4 % 2), i % 4
                        wait_drained(pe, a, fill=part)
                        pe.wait_ge(k_lo_done, 2 * a + m + 1)
                        pe.wait_ge(q_lo_done, 4 * a + 2 * m + 2)
                        rows = slice(32 * g, 32 * g + 32)
                        for j in range(2):
                            cs = slice((c0 + j) * P, (c0 + j + 1) * P)
                            last = product(bk[:, j * 2 * P:(j + 1) * 2 * P].rearrange("p (h q) -> p h q", h=2),
                                           (k_hi[rows, m, cs], k_lo[rows, m, cs]),
                                           (q_hi[rows, m, :, cs], q_lo[rows, m, :, cs]), True, True)
                        last.then_inc(filled, 1)
                    elif name == "values":
                        j, g = i // 4, i % 4
                        m = j // 2
                        wait_drained(pe, a, ("scores", i), ("v", j % 2))
                        if j % 2 == 0:
                            wait(pe, num_done, 2 * a + m)
                        for c in (2 * (j % 2), 2 * (j % 2) + 1):
                            for h in range(2):
                                last = nc.tensor.matmul(
                                    o_bank[32 * g:32 * g + 32, c * P:(c + 1) * P],
                                    v_win[:, c, 4 * m + g, h:h + 2, :].rearrange("p t d -> p (t d)"),
                                    scores[:, i % SM, 2 * (c % 2) + h, :],
                                    start=(c == 0 and h == 0), stop=False, skip_group_check=True)
                        last.then_inc(values_done, 1)
                    elif name == "inter":
                        m = i // 2
                        for c in ((1,), (2, 3))[i % 2]:
                            if c == 1:
                                wait_drained(pe, a, ("state", m * SUBS + 1))
                            else:
                                pe.wait_ge(state_done, 4 * a + 2 * m + c - 1)
                            last = nc.tensor.matmul(o_bank[:, c * P:(c + 1) * P], st[:, c - 1, :],
                                                    qf[:, m, c * P:(c + 1) * P], start=False, stop=True,
                                                    skip_group_check=True)
                        if i % 2 == 1:
                            last.then_inc(o_filled, 1)
                    elif name == "den_turn":
                        wait_drained(pe, a, fill=part)
                        pe.wait_ge(qk_done, 2 * a + i + 1)
                        for s in range(SUBS):
                            last = nc.tensor.transpose(bk[:, s * P:(s + 1) * P], expo[:, i, s * P:(s + 1) * P], ident)
                        last.then_inc(filled, 1)
                    elif name == "spread":
                        wait_drained(pe, a, fill=part)
                        pe.wait_ge(rden_wide, 2 * a + i + 1)
                        for s in range(SUBS):
                            last = nc.tensor.transpose(bk[:, s * P:(s + 1) * P], expo[:, i, s * P:(s + 1) * P], ident)
                        last.then_inc(filled, 1)
                    elif name == "router":
                        wait_drained(pe, a, ("turn", 2), ("turn", 3), fill=part)
                        if isinstance(a, int) and a == 0:
                            pe.wait_ge(split_lo, NP + 1)
                        for s in range(SUBS):
                            ss = slice(s * P, (s + 1) * P)
                            dst = bk[:, s * 2 * E:(s + 1) * 2 * E]
                            for kc in range(KC):
                                nc.tensor.matmul(dst, XA[0][:, kc, ss],
                                                 wr_parts[:, kc, :, :].rearrange("p t e -> p (t e)"),
                                                 start=(s == 0 and kc == 0), stop=False, skip_group_check=True)
                                last = nc.tensor.matmul(dst[:, 0:E], XA[1][:, kc, ss], wr_parts[:, kc, 0, :],
                                                        start=False, stop=(kc == KC - 1), skip_group_check=True)
                        last.then_inc(filled, 1)
                    elif name == "weights_turn":
                        wait_drained(pe, a, fill=part)
                        pe.wait_ge(cw_ready, a + 1)
                        nc.tensor.transpose(bk[0:E * SUBS, 0:P], cw[:, :, :].rearrange("p e s -> p (e s)"), ident)\
                            .then_inc(filled, 1)

            run(step, pe)


CHAIN_NORM = 3
CHAIN_A = 2 * CHAIN_NORM + 2 + 16
C_IDENT = 0
C_CAUSAL = C_IDENT + P
C_BLOCK = C_CAUSAL + P
C_EO = C_BLOCK + P
C_TIE_E = C_EO + 2
C_TIE_G = C_TIE_E + E * E
C_POW = C_TIE_G + GROUPS * GROUPS
C_ONE = C_POW + SUBS
CONST_COLS = C_ONE + 1


def constants():
    c = np.zeros((P, CONST_COLS), np.float32)
    p = np.arange(P)
    c[:, C_IDENT:C_IDENT + P] = np.eye(P)
    c[:, C_CAUSAL:C_CAUSAL + P] = p[None, :] >= p[:, None]
    c[:, C_BLOCK:C_BLOCK + P] = (p[:, None] // DH) == (p[None, :] // DH)
    c[:, C_EO] = (p // DH) % 2 == 0
    c[:, C_EO + 1] = (p // DH) % 2 == 1
    for at, n in ((C_TIE_E, E), (C_TIE_G, GROUPS)):
        c[:, at:at + n * n] = (np.arange(n)[None, :] < np.arange(n)[:, None]).reshape(-1)
    c[:, C_POW:C_POW + SUBS] = -0.5
    c[:, C_ONE] = 1.0
    return c


def kernel(**inputs):
    import concourse.bacc as bacc
    from concourse.bass_utils import run_bass_kernel_spmd

    g = {k.removeprefix("L0_"): np.asarray(v) for k, v in inputs.items()}
    qkvo = np.concatenate([g["attn_" + n].T for n in ("Wq", "Wk", "Wv", "Wo")], axis=1)
    gate = np.concatenate([g["ffn_Wg_s"][None], g["ffn_Wg"]])
    up = np.concatenate([g["ffn_Wu_s"][None], g["ffn_Wu"]])
    down = np.concatenate([g["ffn_Wd_s"][None], g["ffn_Wd"]])
    gu = np.stack([gate, up], axis=1).reshape(SLOTS, 2, KC, P, FF).transpose(3, 0, 1, 2, 4)
    arrays = {
        "x": g["attn_x"],
        "w_qkvo": qkvo.reshape(KC, P, 4 * D).transpose(1, 0, 2),
        "w_gate_up": gu.reshape(P, SLOTS * 2 * KC * FF),
        "w_down": down.transpose(1, 0, 2).reshape(P, SLOTS * D),
        "w_router": g["ffn_gate_w"].T.reshape(KC, P, E).transpose(1, 0, 2),
        "bias": g["ffn_correction_bias"],
        "consts": constants(),
    }
    nc = bacc.Bacc("TRN2", target_bir_lowering=False, num_devices=1)
    ins, args = {}, []
    for name, v in arrays.items():
        v = np.ascontiguousarray(v)
        ins[f"in_{name}"] = v
        args.append(nc.dram_tensor(f"in_{name}", v.shape, mybir.dt.from_np(v.dtype), kind="ExternalInput").ap())
    args.append(nc.dram_tensor("out_y", (B, S, D), mybir.dt.float32, kind="ExternalOutput").ap())
    linear_attention_moe(nc, *args)
    r = run_bass_kernel_spmd(nc, [ins], core_ids=[0])
    return r.results[0]["out_y"]
```

```python
import concourse.bass as bass
from concourse import mybir
from contextlib import ExitStack
import numpy as np

B, S, D = 16, 512, 256
H, DH = 16, 16
E, FF = 8, 128
GROUPS, TOP_GROUPS, TOP_K = 4, 2, 4
ROUTE_SCALE = 2.5
LN_EPS, ATT_EPS, ROUTE_EPS = 1e-5, 1e-8, 1e-20

P = 128
SUBS = S // P
KC = D // P
MH = P // DH
PAIRS = H // 2
PER_G = E // GROUPS
SLOTS = E + 1

ET, HR, CW, SM, GB = 3, 3, 4, 8, 3

SCHEDULE = [
    ("rank", 0), ("finish", 0), ("rank", 1), ("gate", 0), ("turn", 0), ("up", 0), ("turn", 1),
    ("split", 0), ("weights_turn", 0), ("gate", 1), ("result", 0), ("k", 0), ("q", 0), ("k", 1),
    ("q", 1), ("k_split", 0), ("cum", 0), ("up", 1), ("q_split", 0), ("v", 0), ("gate", 2),
    ("k_turn", 0), ("k_split", 1), ("v", 1), ("q_split", 1), ("down", 0), ("k_turn", 1),
    ("state", 0), ("up", 2), ("scores", 0), ("split", 1), ("cum", 1), ("split", 2), ("down", 1),
    ("scores", 1), ("gate", 3), ("scores", 2), ("values", 0), ("inter", 0), ("scores", 3),
    ("up", 3), ("den_turn", 0), ("den_turn", 1), ("down", 2), ("values", 1), ("scores", 4),
    ("gate", 4), ("split", 3), ("inter", 1), ("scores", 5), ("up", 4), ("state", 1), ("gate", 5),
    ("split", 4), ("scores", 6), ("down", 3), ("up", 5), ("scores", 7), ("values", 2),
    ("spread", 0), ("inter", 2), ("values", 3), ("inter", 3), ("spread", 1), ("gate", 6), ("up", 6),
    ("split", 5), ("gate", 7), ("wo", 0), ("wo", 1), ("down", 4), ("down", 5), ("ln2_stats", 0),
    ("split", 6), ("up", 7), ("ln2_apply", 0), ("split", 7), ("gate", 8), ("turn", 2), ("turn", 3),
    ("up", 8), ("ln1_stats", 0), ("split", 8), ("down", 6), ("router", 0), ("route", 0),
    ("down", 7), ("ln1_apply", 0),
]
FIRST_NORM = [("ln1_stats", 0), ("ln1_apply", 0)]
ATTENTION = [
    ("turn", 0), ("turn", 1), ("k", 0), ("q", 0), ("k", 1), ("k_split", 0), ("v", 0), ("q", 1),
    ("q_split", 0), ("k_split", 1), ("k_turn", 0), ("v", 1), ("scores", 0), ("k_turn", 1),
    ("cum", 0), ("q_split", 1), ("scores", 1), ("cum", 1), ("state", 0), ("den_turn", 0),
    ("values", 0), ("scores", 2), ("inter", 0), ("scores", 3), ("scores", 4), ("den_turn", 1),
    ("values", 1), ("scores", 5), ("inter", 1), ("state", 1), ("spread", 0), ("values", 2),
    ("scores", 6), ("scores", 7), ("inter", 2), ("values", 3), ("inter", 3), ("spread", 1),
    ("wo", 0), ("wo", 1), ("ln2_stats", 0), ("ln2_apply", 0), ("ln1_stats", 0), ("turn", 2),
    ("turn", 3), ("router", 0), ("route", 0), ("ln1_apply", 0),
]
EXPERTS = [
    ("rank", 0), ("finish", 0), ("rank", 1), ("gate", 0), ("up", 0), ("weights_turn", 0),
    ("result", 0), ("split", 0), ("gate", 1), ("up", 1), ("gate", 2), ("up", 2), ("down", 0),
    ("split", 1), ("split", 2), ("gate", 3), ("up", 3), ("gate", 4), ("split", 3), ("down", 1),
    ("down", 2), ("up", 4), ("gate", 5), ("split", 4), ("up", 5), ("gate", 6), ("down", 3),
    ("up", 6), ("split", 5), ("gate", 7), ("split", 6), ("up", 7), ("gate", 8), ("up", 8),
    ("down", 4), ("split", 7), ("down", 5), ("down", 6), ("down", 7), ("split", 8),
]
BANKED = ("turn", "v", "k", "q", "k_turn", "state", "scores", "den_turn", "spread", "wo")


def fills(part):
    name, i = part
    return [(name, 2 * i), (name, 2 * i + 1)] if name == "scores" else [part]


FINISH = [("finish", 0), ("result", 0)]
FIRST_STEP = [x for x in SCHEDULE if x not in FINISH]


def numbered(parts):
    return {u: n for n, u in enumerate(u for x in parts if x[0] in BANKED for u in fills(x))}


USE, FIRST_USE = numbered(SCHEDULE), numbered(ATTENTION)
USES = len(USE)
assert USES % 2 == 0 and set(FIRST_USE) == set(USE)


def linear_attention_moe(nc, x, w_qkvo, w_gate_up, w_down, w_router, bias, consts, out):
    f32, f32r = mybir.dt.float32, mybir.dt.float32r
    ALU, ACT, AX = mybir.AluOpType, mybir.ActivationFunctionType, mybir.AxisListType

    ctx = ExitStack()
    with ctx:
        def sb(name, shape, dt=f32):
            return ctx.enter_context(nc.sbuf_tensor(name, shape, dt))

        def ps(name, shape):
            return ctx.enter_context(nc.psum_tensor(name, shape, f32))

        def sem(name):
            return ctx.enter_context(nc.semaphore(name))

        wa_hi, wa_lo = (sb(f"wa_{n}", [P, KC, 4 * D], f32r) for n in ("hi", "lo"))
        wg_hi, wg_lo = (sb(f"wg_{n}", [P, SLOTS, 2, KC, FF], f32r) for n in ("hi", "lo"))
        wd_hi, wd_lo = (sb(f"wd_{n}", [P, SLOTS, D], f32r) for n in ("hi", "lo"))
        wr_parts = sb("wr_parts", [P, KC, 2, E], f32r)
        wr_raw = sb("wr_raw", [P, KC, E])
        bias_sb = sb("bias_sb", [P, E])
        cst = sb("cst", [P, CONST_COLS])
        ident = cst[:, C_IDENT:C_IDENT + P]
        causal = cst[:, C_CAUSAL:C_CAUSAL + P]
        block_mask = cst[:, C_BLOCK:C_BLOCK + P]
        one = cst[:, C_ONE:C_ONE + 1]
        before_e = cst[:, C_TIE_E:C_TIE_E + E * E].rearrange("p (a b) -> p a b", a=E)
        before_g = cst[:, C_TIE_G:C_TIE_G + GROUPS * GROUPS].rearrange("p (a b) -> p a b", a=GROUPS)
        power = cst[:, C_POW:C_POW + SUBS]

        x_in = sb("x_in", [P, SUBS, D])
        x_mid = [sb(f"x_mid{i}", [P, SUBS, D]) for i in range(2)]
        norm1 = sb("norm1", [P, SUBS, D])
        at_hi, at_lo = (sb(f"at_{n}", [P, KC, S], f32r) for n in ("hi", "lo"))
        num_t = sb("num_t", [P, KC, S])
        norm2 = num_t[:, :, :].rearrange("p k (a d) -> p (k a) d", d=D)
        xt_hi, xt_lo = ([sb(f"xt_{n}{i}", [P, KC, S], f32r) for i in range(2)] for n in ("hi", "lo"))
        kf, qf = sb("kf", [P, KC, S]), sb("qf", [P, KC, S])
        expo = sb("expo", [P, 2, S])
        k_hi, k_lo = (sb(f"k_{n}", [P, KC, S], f32r) for n in ("hi", "lo"))
        q_hi, q_lo = (sb(f"q_{n}", [P, KC, 2, S], f32r) for n in ("hi", "lo"))
        k_tok = sb("k_tok", [P, KC, SUBS - 1, P])
        v_win = sb("v_win", [P, SUBS, PAIRS, 3, DH])
        scores = sb("scores", [P, SM, 4, P])
        st = sb("st", [P, SUBS - 1, P])
        den = sb("den", [P, SUBS, MH])
        rden = sb("rden", [P, KC, SUBS, MH])
        stats = sb("stats", [P, SUBS, 6])
        m_sum, m_dif, v_sum, mean, minus_mean = (
            sb(n, [P, SUBS]) for n in ("m_sum", "m_dif", "v_sum", "mean", "minus_mean"))
        veps = sb("veps", [P, SUBS])
        rstd = sb("rstd", [P, SUBS])
        shift = sb("shift", [P, SUBS])
        spare = num_t[:, :, :].rearrange("p k n -> p (k n)")

        def compared(at, n):
            c, q = at + SUBS * n * 2 * n, SUBS * n * n
            return (spare[:, at:c].rearrange("p (s a t b) -> p s a t b", s=SUBS, a=n, t=2),
                    spare[:, c:c + q].rearrange("p (s a b) -> p s a b", s=SUBS, a=n))

        e_cmp, e_eq = compared(0, E)
        g_cmp, g_eq = compared(3 * SUBS * E * E, GROUPS)
        logit = sb("logit", [P, SUBS, E])
        sig = sb("sig", [P, SUBS, E])
        sig_c = sb("sig_c", [P, SUBS, E])
        g_sum = sb("g_sum", [P, SUBS, GROUPS])
        g_rank = sb("g_rank", [P, SUBS, GROUPS])
        choice = sb("choice", [P, SUBS, E])
        e_rank = sb("e_rank", [P, SUBS, E])
        w_sel = sb("w_sel", [P, SUBS, E])
        w_sum = sb("w_sum", [P, SUBS])
        w_rec = sb("w_rec", [P, SUBS])
        cw = sb("cw", [P, E, SUBS])
        cw_t = sb("cw_t", [E * SUBS, P])
        cw_all = sb("cw_all", [P, CW, S])
        stage = cw_all[:, :, :].rearrange("p (a s) n -> p a (s n)", a=2)
        et = sb("et", [P, ET, S])
        h_hi, h_lo = (sb(f"h_{n}", [P, HR, S], f32r) for n in ("hi", "lo"))

        bank = [ps(f"bank{i}", [P, S]) for i in range(2)]
        o_bank = ps("o_bank", [P, S])
        g_bank = [ps(f"g_bank{i}", [P, S]) for i in range(GB)]
        y_bank = [ps(f"y_bank{i}", [P, 2, D]) for i in range(2)]
        cw_dram = nc.dram_tensor("cw_dram", [2, E, S], f32, kind="Internal").ap()

        x_v = x.rearrange("b (s p) d -> b p s d", p=P)
        out_v = out.rearrange("b (s p) d -> b p s d", p=P)

        staged = [sem(f"staged{i}") for i in range(2)]
        small_in = sem("small_in")
        split_hi = sem("split_hi")
        split_lo = sem("split_lo")
        zeros_set = sem("zeros_set")
        x_loaded = sem("x_loaded")
        filled = sem("filled")
        drained = [sem(f"drained{i}") for i in range(2)]
        turn_hi = sem("turn_hi")
        relu_done = sem("relu_done")
        exp_done = sem("exp_done")
        k_hi_done, k_lo_done = sem("k_hi_done"), sem("k_lo_done")
        q_hi_done, q_lo_done = sem("q_hi_done"), sem("q_lo_done")
        state_done = sem("state_done")
        values_done = sem("values_done")
        o_filled = sem("o_filled")
        num_done = sem("num_done")
        cum_done = sem("cum_done")
        qk_done = sem("qk_done")
        rden_done = sem("rden_done")
        rden_wide = sem("rden_wide")
        att_hi_done, att_lo_done = sem("att_hi_done"), sem("att_lo_done")
        var_ready, rstd_ready = sem("var_ready"), sem("rstd_ready")
        shift_ready = sem("shift_ready")
        norm_ready = sem("norm_ready")
        expn_done = sem("expn_done")
        cw_ready = sem("cw_ready")
        router_filled, logit_ready = sem("router_filled"), sem("logit_ready")
        cwt_filled, cwt_ready = sem("cwt_filled"), sem("cwt_ready")
        cw_stored = sem("cw_stored")
        cw_loaded = [sem(f"cw_loaded{i}") for i in range(CW)]
        cw_used = sem("cw_used")
        g_filled = sem("g_filled")
        g_drained = sem("g_drained")
        tanh_done = sem("tanh_done")
        h_hi_done, h_lo_done = sem("h_hi_done"), sem("h_lo_done")
        down_done = sem("down_done")
        y_drained = sem("y_drained")
        out_sent = [sem(f"out_sent{i}") for i in range(2)]
        chain = sem("chain")

        def wait(eng, s, value):
            if isinstance(value, int) and value <= 0:
                return
            eng.wait_ge(s, value)

        def nth(b, use):
            return (FIRST_USE if isinstance(b, int) and b == 0 else USE)[use]

        def wait_filled(eng, b, part):
            eng.wait_ge(filled, USES * b + nth(b, part) + 1)

        def wait_drained(eng, b, *parts, fill=None):
            need = [0, 0]
            for part in parts:
                n = nth(b, part)
                need[n % 2] = max(need[n % 2], n // 2 + 1)
            new = [nth(b, u) for u in fills(fill)] if fill else []
            for n in new:
                need[n % 2] = max(need[n % 2], n // 2)
            for j in range(2):
                if need[j] or j in [n % 2 for n in new]:
                    wait(eng, drained[j], USES // 2 * b + need[j])

        def bank_of(b, part):
            return bank[nth(b, part) % 2]

        def run(step, eng):
            step(FIRST_NORM, -2, -1, 0)
            step(ATTENTION, -1, -1, 1)
            step(FIRST_STEP, 0, 0, 0)
            with eng.Fori(0, (B - 2) // 2) as k:
                step(SCHEDULE, k * 2 + 1, k, 1)
                step(SCHEDULE, k * 2 + 2, k + 1, 0)
            step(EXPERTS, B - 1, (B - 1) // 2, 1)
            step(FINISH, B, B // 2, 0)

        PIECES = []
        for kc in range(KC):
            PIECES.append((w_qkvo[:, kc], 4 * D, wa_hi[:, kc], wa_lo[:, kc]))
        GU = 2 * KC * FF
        for s in range(0, SLOTS, 2):
            n = min(2, SLOTS - s)
            PIECES.append((w_gate_up[:, s * GU:(s + n) * GU], n * GU,
                           wg_hi[:, s:s + n].rearrange("p s g k f -> p (s g k f)"),
                           wg_lo[:, s:s + n].rearrange("p s g k f -> p (s g k f)")))
        for s in range(0, SLOTS, 4):
            n = min(4, SLOTS - s)
            PIECES.append((w_down[:, s * D:(s + n) * D], n * D,
                           wd_hi[:, s:s + n].rearrange("p s n -> p (s n)"),
                           wd_lo[:, s:s + n].rearrange("p s n -> p (s n)")))
        NP = len(PIECES)
        SPLIT_FROM, SPLIT_EVERY = 4, 4

        def piece_before(parts, t):
            n, left = divmod(t - SPLIT_FROM, SPLIT_EVERY)
            return KC + n if parts is ATTENTION and n >= 0 and left == 0 and KC + n <= NP else None

        def low_part(eng, ops, n):
            eng.wait_ge(split_hi, n + 1)
            if n < NP:
                _, cols, hi, lo = PIECES[n]
                ops.tensor_tensor(lo, stage[:, n % 2, 0:cols], hi.bitcast(f32), ALU.subtract)\
                    .then_inc(split_lo, 1)
            else:
                ops.tensor_tensor(wr_parts[:, :, 1, :], wr_raw[:, :, :], wr_parts[:, :, 0, :].bitcast(f32),
                                  ALU.subtract).then_inc(split_lo, 1)

        block = ctx.enter_context(nc.Block())

        @block.sync
        def _(sp):
            def load_x(b):
                sp.dma_start(x_in[:, :, :], x_v[b] if isinstance(b, int) else
                             x_v[bass.ds(b, 1)].rearrange("a p s d -> p (a s) d")).then_inc(x_loaded, 16)

            load_x(0)
            sp.dma_start(cst[:, :], consts).then_inc(small_in, 16)
            sp.dma_start(bias_sb[:, :], bias.partition_broadcast(P)).then_inc(small_in, 16)
            sp.dma_start(wr_raw[:, :, :], w_router).then_inc(small_in, 16)
            for n, (src, cols, _, _) in enumerate(PIECES):
                if n >= 2:
                    sp.wait_ge(split_lo, n - 1)
                sp.dma_start(stage[:, n % 2, 0:cols], src).then_inc(staged[n % 2], 16)

            def step(parts, b, half, parity):
                a, pa = b + 1, 1 - parity
                for name, i in parts:
                    if name == "down" and i < E - CW:
                        load_cw(b, parity, i + CW)
                    elif name == "ln2_stats":
                        wait_drained(sp, a, ("wo", 1))
                        next_x(a)
                    elif name == "weights_turn":
                        sp.wait_ge(cwt_ready, b + 1)
                        sp.dma_start(cw_dram[parity].rearrange("e (s p) -> (e s) p", p=P), cw_t[:, :])\
                            .then_inc(cw_stored, 16)
                        if isinstance(b, int) and b == 0:
                            sp.wait_ge(split_lo, NP)
                        for e in range(CW):
                            load_cw(b, parity, e)
                    elif name == "result":
                        sp.wait_ge(y_drained, 2 * b)
                        sp.dma_start(out_v[b - 1] if isinstance(b, int) else
                                     out_v[bass.ds(b - 1, 1)].rearrange("a p s d -> p (a s) d"),
                                     x_mid[pa][:, :, :]).then_inc(out_sent[pa], 16)

            def next_x(a):
                load_x((a + 1) % B)

            def load_cw(b, parity, e):
                if e == 0:
                    sp.wait_ge(cw_stored, 16 * b + 16)
                wait(sp, cw_used, E * b + e - CW + 1)
                sp.dma_start(cw_all[:, e % CW, :], cw_dram[parity, e].partition_broadcast(P))\
                    .then_inc(cw_loaded[e % CW], 16)

            run(step, sp)
            sp.wait_ge(out_sent[0], 16 * (B // 2))
            sp.wait_ge(out_sent[1], 16 * (B // 2))
            sp.wait_ge(x_loaded, 16 * (B + 1))

        @block.scalar
        def _(act):
            def weights_high(n):
                if n < NP:
                    _, cols, hi, _ = PIECES[n]
                    act.wait_ge(staged[n % 2], 16 * (n // 2 + 1))
                    nc.scalar.activation(hi, stage[:, n % 2, 0:cols], ACT.Copy).then_inc(split_hi, 1)
                else:
                    nc.scalar.activation(wr_parts[:, :, 0, :], wr_raw[:, :, :], ACT.Copy).then_inc(split_hi, 1)

            act.wait_ge(small_in, 48)
            for n in range(KC):
                weights_high(n)

            def step(parts, b, half, parity):
                a, pa = b + 1, 1 - parity

                def h_high(e):
                    act.wait_ge(g_drained, 2 * SLOTS * b + 2 * e + 2)
                    wait(act, down_done, SLOTS * b + e - HR + 1)
                    nc.scalar.activation(h_hi[:, e % HR, :], et[:, e % ET, :], ACT.Copy)\
                        .then_inc(h_hi_done, 1)

                for t, (name, i) in enumerate(parts):
                    part = (name, i)
                    if piece_before(parts, t) is not None:
                        weights_high(piece_before(parts, t))
                    if name == "gate":
                        act.wait_ge(g_filled, 2 * SLOTS * b + 2 * i + 1)
                        wait(act, h_lo_done, SLOTS * b + i - ET + 1)
                        nc.scalar.activation(et[:, i % ET, :], g_bank[2 * i % GB][:, :], ACT.Tanh,
                                             scale=0.5).then_inc(tanh_done, 1)
                    elif name == "split":
                        h_high(i)
                    elif name == "turn":
                        wait_filled(act, a, part)
                        dst = at_hi if i < 2 else xt_hi[pa]
                        nc.scalar.activation(dst[:, i % 2, :], bank_of(a, part)[:, :], ACT.Copy)\
                            .then_inc(turn_hi, 1)
                    elif name == "v":
                        if i == 0:
                            act.wait_ge(zeros_set, 1)
                        wait_filled(act, a, part)
                        nc.scalar.activation(v_win[:, 2 * i:2 * i + 2, :, 0:3:2, :]
                                             .rearrange("p s g t d -> p (s g) t d"),
                                             bank_of(a, part)[:, :].rearrange("p (g t d) -> p g t d", t=2, d=DH),
                                             ACT.Copy).then_inc(drained[nth(a, part) % 2], 1)
                    elif name in ("k", "q"):
                        n = 2 * i + (name == "q")
                        wait_filled(act, a, part)
                        if i > 0:
                            wait_drained(act, a, (name, i - 1))
                        nc.scalar.activation(expo[:, n % 2, :], bank_of(a, part)[:, :], ACT.Relu, scale=-1.0)\
                            .then_inc(relu_done, 1)
                        act.wait_ge(relu_done, 4 * a + n + 1)
                        nc.scalar.activation(expo[:, n % 2, :], expo[:, n % 2, :], ACT.Exp, scale=-1.0)\
                            .then_inc(exp_done, 1)
                    elif name == "k_split":
                        wait_drained(act, a, ("k", i))
                        nc.scalar.activation(k_hi[:, i, :], kf[:, i, :], ACT.Copy).then_inc(k_hi_done, 1)
                    elif name == "q_split":
                        wait_drained(act, a, ("q", i))
                        for j in range(2):
                            nc.scalar.activation(q_hi[:, i, j, :], qf[:, i, :], ACT.Copy,
                                                 scale=cst[:, C_EO + j:C_EO + j + 1]).then_inc(q_hi_done, 1)
                    elif name == "k_turn":
                        wait_filled(act, a, part)
                        nc.scalar.activation(k_tok[:, i, :, :].rearrange("p c d -> p (c d)"),
                                             bank_of(a, part)[:, 0:(SUBS - 1) * P], ACT.Copy)\
                            .then_inc(drained[nth(a, part) % 2], 1)
                    elif name == "den_turn":
                        act.wait_ge(rden_done, 2 * a + i + 1)
                        nc.scalar.activation(expo[:, i, :].rearrange("p (a d) -> p a d", d=DH),
                                             rden[:, i, :, :].rearrange("p s h -> p (s h)").unsqueeze(2)
                                             .broadcast_to([P, S // DH, DH]), ACT.Copy).then_inc(rden_wide, 1)
                    elif name == "inter" and i % 2 == 1:
                        act.wait_ge(o_filled, 2 * a + i // 2 + 1)
                        nc.scalar.activation(num_t[:, i // 2, :], o_bank[:, :], ACT.Copy).then_inc(num_done, 1)
                    elif name == "spread":
                        wait_drained(act, a, part)
                        nc.scalar.activation(at_hi[:, i, :], num_t[:, i, :], ACT.Copy).then_inc(att_hi_done, 1)
                    elif name == "ln1_apply" and parts is not FIRST_NORM:
                        act.wait_ge(shift_ready, a + 2)
                        for s in range(SUBS):
                            last = nc.scalar.activation(norm1[:, s, :], x_in[:, s, :], ACT.Identity,
                                                        scale=rstd[:, s:s + 1], bias=shift[:, s:s + 1])
                        last.then_inc(norm_ready, 1)
                    elif name == "route":
                        act.wait_ge(logit_ready, a + 1)
                        nc.scalar.activation(sig[:, :, :], logit[:, :, :], ACT.Exp, scale=-1.0)\
                            .then_inc(expn_done, 1)
                    elif name == "weights_turn":
                        act.wait_ge(cwt_filled, b + 1)
                        wait(act, cw_stored, 16 * b)
                        nc.scalar.activation(cw_t[:, :], o_bank[0:E * SUBS, 0:P], ACT.Copy)\
                            .then_inc(cwt_ready, 1)

            run(step, act)

        @block.gpsimd
        def _(pool):
            nc.gpsimd.memset(v_win[:, :, :, 1, :], 0.0).then_inc(zeros_set, 1)
            pool.wait_ge(small_in, 48)

            def step(parts, b, half, parity):
                a = b + 1

                def weigh(e):
                    if e == 0:
                        return
                    r = (e - 1) % CW
                    pool.wait_ge(cw_loaded[r], 16 * (E // CW * b + (e - 1) // CW + 1))
                    pool.wait_ge(g_drained, 2 * SLOTS * b + 2 * e + 1)
                    nc.gpsimd.tensor_tensor(et[:, e % ET, :], et[:, e % ET, :], cw_all[:, r, :], ALU.mult)\
                        .then_inc(cw_used, 1)

                def h_low(e):
                    pool.wait_ge(h_hi_done, SLOTS * b + e + 1)
                    nc.gpsimd.tensor_tensor(h_lo[:, e % HR, :], et[:, e % ET, :],
                                            h_hi[:, e % HR, :].bitcast(f32), ALU.subtract)\
                        .then_inc(h_lo_done, 1)

                if parts is ATTENTION:
                    pool.wait_ge(split_lo, KC)
                for t, (name, i) in enumerate(parts):
                    if piece_before(parts, t) is not None:
                        low_part(pool, nc.gpsimd, piece_before(parts, t))
                    if name == "gate":
                        weigh(i)
                    elif name == "split":
                        h_low(i)
                    elif name == "k_split":
                        pool.wait_ge(k_hi_done, 2 * a + i + 1)
                        nc.gpsimd.tensor_tensor(k_lo[:, i, :], kf[:, i, :], k_hi[:, i, :].bitcast(f32),
                                                ALU.subtract).then_inc(k_lo_done, 1)
                    elif name == "cum":
                        pool.wait_ge(cum_done, 2 * a + i + 1)
                        nc.gpsimd.tensor_tensor(expo[:, i, :], expo[:, i, :], qf[:, i, :], ALU.mult)\
                            .then_inc(qk_done, 1)
                    elif name in ("ln1_apply", "ln2_apply"):
                        pool.wait_ge(var_ready, 2 * a + (3 if name == "ln1_apply" else 2))
                        nc.gpsimd.tensor_tensor(rstd[:, :], veps[:, :], power, ALU.pow)\
                            .then_inc(rstd_ready, 1)
                        if name == "ln1_apply":
                            pool.wait_ge(rstd_ready, 2 * a + 3)
                            nc.gpsimd.tensor_tensor(shift[:, :], minus_mean[:, :], rstd[:, :], ALU.mult)\
                                .then_inc(shift_ready, 1)

            run(step, pool)

        @block.vector
        def _(dve):
            dve.wait_ge(small_in, 48)

            pair = sig_c[:, :, :].rearrange("p s (g t) -> p s g t", t=PER_G)

            def step(parts, b, half, parity):
                a, pa = b + 1, 1 - parity
                own = [0 if parts is FIRST_NORM else CHAIN_NORM if parts is ATTENTION
                       else CHAIN_A * a + CHAIN_NORM - CHAIN_RANK]

                def link(ins):
                    own[0] += 1
                    ins.then_inc(chain, 1)
                    dve.wait_ge(chain, own[0])

                def layernorm_stats(src, n):
                    wait(dve, norm_ready, n - 1)
                    for s in range(SUBS):
                        last = nc.vector.bn_stats(stats[:, s, :], src[:, s, :])
                    link(last)
                    m0, m1, v0, v1 = (stats[:, :, j] for j in (1, 4, 2, 5))
                    nc.vector.tensor_tensor(m_sum[:, :], m0, m1, ALU.add)
                    nc.vector.tensor_tensor(m_dif[:, :], m0, m1, ALU.subtract)
                    link(nc.vector.tensor_tensor(v_sum[:, :], v0, v1, ALU.add))
                    nc.vector.tensor_scalar(mean[:, :], m_sum[:, :], 0.5, None, ALU.mult)
                    nc.vector.scalar_tensor_tensor(m_dif[:, :], m_dif[:, :], 0.25, m_dif[:, :],
                                                   ALU.mult, ALU.mult)
                    link(nc.vector.tensor_scalar(v_sum[:, :], v_sum[:, :], 1.0 / D, LN_EPS, ALU.mult, ALU.add))
                    nc.vector.tensor_scalar(minus_mean[:, :], m_sum[:, :], -0.5, None, ALU.mult)
                    nc.vector.tensor_tensor(veps[:, :], m_dif[:, :], v_sum[:, :], ALU.add)\
                        .then_inc(var_ready, 1)

                def layernorm_apply(src, norm, n):
                    dve.wait_ge(rstd_ready, n)
                    for s in range(SUBS):
                        last = nc.vector.tensor_scalar(norm[:, s, :], src[:, s, :], mean[:, s:s + 1],
                                                       rstd[:, s:s + 1], ALU.subtract, ALU.mult)
                    last.then_inc(norm_ready, 1)

                def beaten(values, n, cmp, eq, before, rank):
                    other = values.unsqueeze(2).broadcast_to([P, SUBS, n, n])
                    own_v = values.unsqueeze(3).broadcast_to([P, SUBS, n, n])
                    nc.vector.tensor_tensor(cmp[:, :, :, 0, :], other, own_v, ALU.is_gt)
                    link(nc.vector.tensor_tensor(eq[:, :, :, :], other, own_v, ALU.is_equal))
                    link(nc.vector.tensor_tensor(cmp[:, :, :, 1, :], eq[:, :, :, :],
                                                 before.unsqueeze(1).broadcast_to([P, SUBS, n, n]),
                                                 ALU.mult))
                    link(nc.vector.tensor_reduce(rank[:, :, :],
                                                 cmp[:, :, :, :, :].rearrange("p s a t b -> p (s a) (t b)"),
                                                 AX.X, ALU.add))

                if parts is ATTENTION:
                    for n in range(KC):
                        low_part(dve, nc.vector, n)
                for name, i in parts:
                    part = (name, i)
                    if name == "gate":
                        dve.wait_ge(tanh_done, SLOTS * b + i + 1)
                        nc.vector.scalar_tensor_tensor(et[:, i % ET, :], et[:, i % ET, :], 1.0,
                                                       g_bank[2 * i % GB][:, :], ALU.add, ALU.mult)\
                            .then_inc(g_drained, 1)
                    elif name == "up":
                        dve.wait_ge(g_filled, 2 * SLOTS * b + 2 * i + 2)
                        if i == 0:
                            dve.wait_ge(g_drained, 2 * SLOTS * b + 1)
                        else:
                            dve.wait_ge(cw_used, E * b + i)
                        nc.vector.scalar_tensor_tensor(et[:, i % ET, :], et[:, i % ET, :], 0.5,
                                                       g_bank[(2 * i + 1) % GB][:, :], ALU.mult, ALU.mult)\
                            .then_inc(g_drained, 1)
                    elif name == "result":
                        dve.wait_ge(down_done, SLOTS * b)
                        for j in range(2):
                            xm = x_mid[pa][:, 2 * j:2 * j + 2, :]
                            nc.vector.tensor_tensor(xm, xm, y_bank[j][:, :, :], ALU.add)\
                                .then_inc(y_drained, 1)
                    elif name == "ln1_stats":
                        dve.wait_ge(x_loaded, 16 * a + 32)
                        layernorm_stats(x_in, 2 * a + 3)
                    elif name == "ln1_apply" and parts is FIRST_NORM:
                        layernorm_apply(x_in, norm1, 1)
                    elif name == "ln2_stats":
                        wait_drained(dve, a, ("wo", 0), ("wo", 1))
                        layernorm_stats(x_mid[pa], 2 * a + 2)
                    elif name == "ln2_apply":
                        layernorm_apply(x_mid[pa], norm2, 2 * a + 2)
                    elif name == "turn":
                        dve.wait_ge(turn_hi, 4 * a + i + 1)
                        dst, hi = (at_lo, at_hi) if i < 2 else (xt_lo[pa], xt_hi[pa])
                        nc.vector.tensor_tensor(dst[:, i % 2, :], bank_of(a, part)[:, :],
                                                hi[:, i % 2, :].bitcast(f32), ALU.subtract)\
                            .then_inc(drained[nth(a, part) % 2], 1)
                    elif name in ("k", "q"):
                        n = 2 * i + (name == "q")
                        dve.wait_ge(exp_done, 4 * a + n + 1)
                        dst = kf if name == "k" else qf
                        nc.vector.scalar_tensor_tensor(dst[:, i, :], bank_of(a, part)[:, :], 0.0,
                                                       expo[:, n % 2, :], ALU.max, ALU.add)\
                            .then_inc(drained[nth(a, part) % 2], 1)
                    elif name == "q_split":
                        for j in range(2):
                            dve.wait_ge(q_hi_done, 4 * a + 2 * i + j + 1)
                            nc.vector.scalar_tensor_tensor(q_lo[:, i, j, :], qf[:, i, :],
                                                           cst[:, C_EO + j:C_EO + j + 1],
                                                           q_hi[:, i, j, :].bitcast(f32),
                                                           ALU.mult, ALU.subtract).then_inc(q_lo_done, 1)
                    elif name == "state":
                        wait_filled(dve, a, part)
                        nc.vector.tensor_tensor(st[:, :, :],
                                                bank_of(a, part)[:, 0:(SUBS - 1) * P].rearrange("p (c n) -> p c n", n=P),
                                                block_mask.unsqueeze(1).broadcast_to([P, SUBS - 1, P]), ALU.mult)\
                            .then_inc(drained[nth(a, part) % 2], 1)
                        wait_drained(dve, a, part)
                        for c in (2, 3):
                            if c == 3:
                                dve.wait_ge(state_done, 4 * a + 2 * i + 1)
                            nc.vector.tensor_tensor(st[:, c - 1, :], st[:, c - 2, :], st[:, c - 1, :],
                                                    ALU.add).then_inc(state_done, 1)
                    elif name == "cum":
                        wait_drained(dve, a, ("k", 1), ("q", 1))
                        nc.vector.tensor_tensor_scan(expo[:, i, :], one.broadcast_to([P, S]), kf[:, i, :], 0.0,
                                                     ALU.mult, ALU.add).then_inc(cum_done, 1)
                    elif name == "scores":
                        wait(dve, values_done, 4 * a + i // 2 - 1)
                        for use in fills(part):
                            wait_filled(dve, a, use)
                            nc.vector.tensor_tensor(scores[:, use[1] % SM, :, :],
                                                    bank_of(a, use)[:, :].rearrange("p (h q) -> p h q", h=4),
                                                    causal.unsqueeze(1).broadcast_to([P, 4, P]), ALU.mult)\
                                .then_inc(drained[nth(a, use) % 2], 1)
                    elif name == "den_turn":
                        wait_filled(dve, a, part)
                        nc.vector.tensor_reduce(den[:, :, :].rearrange("p s h -> p (s h)"),
                                                bank_of(a, part)[:, :].rearrange("p (a d) -> p a d", d=DH),
                                                AX.X, ALU.add).then_inc(drained[nth(a, part) % 2], 1)
                        wait_drained(dve, a, part)
                        link(nc.vector.tensor_scalar(den[:, :, :], den[:, :, :], ATT_EPS, None, ALU.add))
                        nc.vector.reciprocal(rden[:, i, :, :], den[:, :, :]).then_inc(rden_done, 1)
                        dve.wait_ge(rden_done, 2 * a + i + 1)
                    elif name == "spread":
                        wait_filled(dve, a, part)
                        dve.wait_ge(num_done, 2 * a + i + 1)
                        nc.vector.tensor_tensor(num_t[:, i, :], num_t[:, i, :], bank_of(a, part)[:, :], ALU.mult)\
                            .then_inc(drained[nth(a, part) % 2], 1)
                        dve.wait_ge(att_hi_done, 2 * a + i + 1)
                        nc.vector.tensor_tensor(at_lo[:, i, :], num_t[:, i, :], at_hi[:, i, :].bitcast(f32),
                                                ALU.subtract).then_inc(att_lo_done, 1)
                    elif name == "wo":
                        wait_filled(dve, a, part)
                        if i == 0:
                            wait(dve, out_sent[pa], 16 * half_of(b, half, parity))
                        nc.vector.tensor_tensor(x_mid[pa][:, 2 * i:2 * i + 2, :],
                                                bank_of(a, part)[:, :].rearrange("p (s d) -> p s d", s=2),
                                                x_in[:, 2 * i:2 * i + 2, :], ALU.add)\
                            .then_inc(drained[nth(a, part) % 2], 1)
                    elif name == "router":
                        dve.wait_ge(router_filled, a + 1)
                        nc.vector.tensor_reduce(
                            logit[:, :, :].rearrange("p s e -> p (s e)"),
                            o_bank[:, 0:SUBS * 2 * E].rearrange("p (s t e) -> p s e t", s=SUBS, t=2),
                            AX.X, ALU.add).then_inc(logit_ready, 1)
                    elif name == "route":
                        dve.wait_ge(expn_done, a + 1)
                        link(nc.vector.tensor_scalar(sig_c[:, :, :], sig[:, :, :], 1.0, None, ALU.add))
                        link(nc.vector.reciprocal(sig[:, :, :], sig_c[:, :, :]))
                        link(nc.vector.tensor_tensor(sig_c[:, :, :], sig[:, :, :],
                                                     bias_sb[:, :].unsqueeze(1).broadcast_to([P, SUBS, E]), ALU.add))
                        link(nc.vector.tensor_tensor(g_sum[:, :, :], pair[:, :, :, 0], pair[:, :, :, 1], ALU.add))
                        beaten(g_sum[:, :, :], GROUPS, g_cmp, g_eq, before_g, g_rank)
                    elif name == "rank" and i == 0:
                        link(nc.vector.tensor_scalar(g_rank[:, :, :], g_rank[:, :, :], TOP_GROUPS - 0.5, None,
                                                     ALU.is_lt))
                        link(nc.vector.tensor_tensor(choice[:, :, :].rearrange("p s (g t) -> p s g t", t=PER_G), pair,
                                                     g_rank[:, :, :].unsqueeze(3)
                                                     .broadcast_to([P, SUBS, GROUPS, PER_G]), ALU.mult))
                        beaten(choice[:, :, :], E, e_cmp, e_eq, before_e, e_rank)
                    elif name == "rank":
                        link(nc.vector.scalar_tensor_tensor(w_sel[:, :, :], e_rank[:, :, :], TOP_K - 0.5,
                                                            sig[:, :, :], ALU.is_lt, ALU.mult))
                        link(nc.vector.tensor_reduce(w_sum[:, :], w_sel[:, :, :], AX.X, ALU.add))
                        link(nc.vector.tensor_scalar(w_sum[:, :], w_sum[:, :], ROUTE_EPS, None, ALU.add))
                        link(nc.vector.reciprocal(w_rec[:, :], w_sum[:, :]))
                        nc.vector.scalar_tensor_tensor(cw[:, :, :].rearrange("p e s -> p s e"), w_sel[:, :, :],
                                                       ROUTE_SCALE,
                                                       w_rec[:, :].unsqueeze(2).broadcast_to([P, SUBS, E]),
                                                       ALU.mult, ALU.mult).then_inc(cw_ready, 1)

                if isinstance(a, int) and "route" in dict(parts):
                    assert own[0] == CHAIN_A * (a + 1) + CHAIN_NORM - CHAIN_RANK

            def half_of(b, half, parity):
                return half + 1 if parity == 1 else half

            run(step, dve)

        @block.tensor
        def _(pe):
            def product(dst, lhs, rhs, first, last, shared=False):
                (lh, ll), (rh, rl) = lhs, rhs
                for n, (l, r) in enumerate(((lh, rh), (lh, rl), (ll, rh))):
                    ins = nc.tensor.matmul(dst, l, r, start=first and n == 0, stop=last and n == 2,
                                           skip_group_check=shared)
                return ins

            def cols(parts, *index):
                return tuple(p[index] for p in parts)

            WA, WG, WD = (wa_hi, wa_lo), (wg_hi, wg_lo), (wd_hi, wd_lo)
            AT = (at_hi, at_lo)
            ALL = slice(None)

            def step(parts, b, half, parity):
                a, pa = b + 1, 1 - parity
                XT, XA = (xt_hi[parity], xt_lo[parity]), (xt_hi[pa], xt_lo[pa])
                for name, i in parts:
                    part = (name, i)
                    if name in ("k", "q", "v") and isinstance(a, int) and a == 0:
                        pe.wait_ge(split_lo, KC)
                    if name in BANKED and name != "scores":
                        bk = bank_of(a, part)
                    if name in ("gate", "up"):
                        n = 2 * i + (name == "up")
                        if i == 0 and name == "gate":
                            wait_drained(pe, b, ("turn", 3))
                        wait(pe, g_drained, 2 * SLOTS * b + n - GB + 1)
                        if isinstance(b, int) and b == 0:
                            pe.wait_ge(split_lo, KC + i // 2 + 1)
                        for kc in range(KC):
                            last = product(g_bank[n % GB][:, :], cols(WG, ALL, i, n % 2, kc, ALL),
                                           cols(XT, ALL, kc, ALL), kc == 0, kc == KC - 1)
                        last.then_inc(g_filled, 1)
                    elif name in ("down", "finish"):
                        if name == "down":
                            pe.wait_ge(h_lo_done, SLOTS * b + i + 1)
                        else:
                            i = SLOTS - 1
                            pe.wait_ge(h_lo_done, SLOTS * b)
                        if i == 0:
                            wait(pe, y_drained, 2 * b)
                        if isinstance(b, int) and b == 0:
                            pe.wait_ge(split_lo, NP if i == SLOTS - 2 else KC + (SLOTS + 1) // 2 + i // 4 + 1)
                        for s in range(SUBS):
                            last = product(y_bank[s // 2][:, s % 2, :],
                                           (h_hi[:, i % HR, s * P:(s + 1) * P], h_lo[:, i % HR, s * P:(s + 1) * P]),
                                           cols(WD, ALL, i, ALL), i == 0 and s % 2 == 0, i == SLOTS - 1, shared=True)
                        last.then_inc(down_done, 1)
                    elif name == "turn":
                        norm = norm1 if i < 2 else norm2
                        if isinstance(a, int) and a == 0 and i == 0:
                            pe.wait_ge(small_in, 48)
                        if i % 2 == 0:
                            pe.wait_ge(norm_ready, 2 * a + i // 2 + 1)
                        wait_drained(pe, a, fill=part)
                        for s in range(SUBS):
                            last = nc.tensor.transpose(bk[:, s * P:(s + 1) * P],
                                                       norm[:, s, (i % 2) * P:(i % 2 + 1) * P], ident)
                        last.then_inc(filled, 1)
                    elif name in ("v", "wo"):
                        if name == "v":
                            wait_drained(pe, a, ("turn", 0), ("turn", 1), fill=part)
                        else:
                            wait_drained(pe, a, fill=part)
                            pe.wait_ge(att_lo_done, 2 * a + 2)
                        w0 = 2 * D if name == "v" else 3 * D
                        for j in range(2):
                            s = 2 * i + j
                            for kc in range(KC):
                                last = product(bk[:, j * D:(j + 1) * D], cols(AT, ALL, kc, slice(s * P, (s + 1) * P)),
                                               cols(WA, ALL, kc, slice(w0, w0 + D)), kc == 0, kc == KC - 1)
                        last.then_inc(filled, 1)
                    elif name in ("k", "q"):
                        w0 = (D if name == "k" else 0) + i * P
                        wait_drained(pe, a, ("turn", 0), ("turn", 1), fill=part)
                        for kc in range(KC):
                            last = product(bk[:, :], cols(WA, ALL, kc, slice(w0, w0 + P)),
                                           cols(AT, ALL, kc, ALL), kc == 0, kc == KC - 1)
                        last.then_inc(filled, 1)
                    elif name == "k_turn":
                        wait_drained(pe, a, ("k", i), fill=part)
                        for c in range(SUBS - 1):
                            last = nc.tensor.transpose(bk[:, c * P:(c + 1) * P], kf[:, i, c * P:(c + 1) * P], ident)
                        last.then_inc(filled, 1)
                    elif name == "state":
                        wait_drained(pe, a, ("k_turn", i), ("v", 0), ("v", 1), fill=part)
                        for c in range(SUBS - 1):
                            last = nc.tensor.matmul(bk[:, c * P:(c + 1) * P].rearrange("p (g t d) -> p g t d", t=2, d=DH),
                                                    k_tok[:, i, c, :], v_win[:, c, i * 4:(i + 1) * 4, 0:3:2, :],
                                                    start=True, stop=True)
                        last.then_inc(filled, 1)
                    elif name == "scores":
                        m, c0 = i // 4, 2 * (i // 2 % 2)
                        wait_drained(pe, a, fill=part)
                        pe.wait_ge(k_lo_done, 2 * a + m + 1)
                        pe.wait_ge(q_lo_done, 4 * a + 2 * m + 2)
                        for j in range(2):
                            cs = slice((c0 + j) * P, (c0 + j + 1) * P)
                            for n, (kp, qp) in enumerate(((k_hi, q_hi), (k_hi, q_lo), (k_lo, q_hi))):
                                for use in fills(part):
                                    g = use[1] % 4
                                    rows = slice(32 * g, 32 * g + 32)
                                    last = nc.tensor.matmul(
                                        bank_of(a, use)[:, j * 2 * P:(j + 1) * 2 * P].rearrange("p (h q) -> p h q", h=2),
                                        kp[rows, m, cs], qp[rows, m, :, cs], start=(n == 0), stop=(n == 2))
                                    if j == 1 and n == 2:
                                        last.then_inc(filled, 1)
                    elif name == "values":
                        m = i // 2
                        wait_drained(pe, a, ("scores", 4 * i + 2), ("scores", 4 * i + 3), ("v", i % 2))
                        if i == 0:
                            wait(pe, cwt_ready, a)
                        elif i == 2:
                            pe.wait_ge(num_done, 2 * a + 1)
                        for c in (2 * (i % 2), 2 * (i % 2) + 1):
                            for h in range(2):
                                for g in range(4):
                                    last = nc.tensor.matmul(
                                        o_bank[32 * g:32 * g + 32, c * P:(c + 1) * P],
                                        v_win[:, c, 4 * m + g, h:h + 2, :].rearrange("p t d -> p (t d)"),
                                        scores[:, (4 * i + g) % SM, 2 * (c % 2) + h, :],
                                        start=(c == 0 and h == 0), stop=False, skip_group_check=True)
                        last.then_inc(values_done, 1)
                    elif name == "inter":
                        m = i // 2
                        for c in ((1,), (2, 3))[i % 2]:
                            if c == 1:
                                wait_drained(pe, a, ("state", m))
                            else:
                                pe.wait_ge(state_done, 4 * a + 2 * m + c - 1)
                            last = nc.tensor.matmul(o_bank[:, c * P:(c + 1) * P], st[:, c - 1, :],
                                                    qf[:, m, c * P:(c + 1) * P], start=False, stop=True,
                                                    skip_group_check=True)
                        if i % 2 == 1:
                            last.then_inc(o_filled, 1)
                    elif name == "den_turn":
                        wait_drained(pe, a, fill=part)
                        pe.wait_ge(qk_done, 2 * a + i + 1)
                        for s in range(SUBS):
                            last = nc.tensor.transpose(bk[:, s * P:(s + 1) * P], expo[:, i, s * P:(s + 1) * P], ident)
                        last.then_inc(filled, 1)
                    elif name == "spread":
                        wait_drained(pe, a, fill=part)
                        pe.wait_ge(rden_wide, 2 * a + i + 1)
                        for s in range(SUBS):
                            last = nc.tensor.transpose(bk[:, s * P:(s + 1) * P], expo[:, i, s * P:(s + 1) * P], ident)
                        last.then_inc(filled, 1)
                    elif name == "router":
                        wait_drained(pe, a, ("turn", 2), ("turn", 3))
                        pe.wait_ge(num_done, 2 * a + 2)
                        if isinstance(a, int) and a == 0:
                            pe.wait_ge(split_lo, NP + 1)
                        for s in range(SUBS):
                            ss = slice(s * P, (s + 1) * P)
                            dst = o_bank[:, s * 2 * E:(s + 1) * 2 * E]
                            for kc in range(KC):
                                nc.tensor.matmul(dst, XA[0][:, kc, ss],
                                                 wr_parts[:, kc, :, :].rearrange("p t e -> p (t e)"),
                                                 start=(s == 0 and kc == 0), stop=False, skip_group_check=True)
                                last = nc.tensor.matmul(dst[:, 0:E], XA[1][:, kc, ss], wr_parts[:, kc, 0, :],
                                                        start=False, stop=(kc == KC - 1), skip_group_check=True)
                        last.then_inc(router_filled, 1)
                    elif name == "weights_turn":
                        pe.wait_ge(cw_ready, b + 1)
                        nc.tensor.transpose(o_bank[0:E * SUBS, 0:P], cw[:, :, :].rearrange("p e s -> p (e s)"), ident)\
                            .then_inc(cwt_filled, 1)

            run(step, pe)


CHAIN_NORM = 3
CHAIN_RANK = 9
CHAIN_A = 2 * CHAIN_NORM + 2 + 16
C_IDENT = 0
C_CAUSAL = C_IDENT + P
C_BLOCK = C_CAUSAL + P
C_EO = C_BLOCK + P
C_TIE_E = C_EO + 2
C_TIE_G = C_TIE_E + E * E
C_POW = C_TIE_G + GROUPS * GROUPS
C_ONE = C_POW + SUBS
CONST_COLS = C_ONE + 1


def constants():
    c = np.zeros((P, CONST_COLS), np.float32)
    p = np.arange(P)
    c[:, C_IDENT:C_IDENT + P] = np.eye(P)
    c[:, C_CAUSAL:C_CAUSAL + P] = p[None, :] >= p[:, None]
    c[:, C_BLOCK:C_BLOCK + P] = (p[:, None] // DH) == (p[None, :] // DH)
    c[:, C_EO] = (p // DH) % 2 == 0
    c[:, C_EO + 1] = (p // DH) % 2 == 1
    for at, n in ((C_TIE_E, E), (C_TIE_G, GROUPS)):
        c[:, at:at + n * n] = (np.arange(n)[None, :] < np.arange(n)[:, None]).reshape(-1)
    c[:, C_POW:C_POW + SUBS] = -0.5
    c[:, C_ONE] = 1.0
    return c


def kernel(**inputs):
    import concourse.bacc as bacc
    from concourse.bass_utils import run_bass_kernel_spmd

    g = {k.removeprefix("L0_"): np.asarray(v) for k, v in inputs.items()}
    qkvo = np.concatenate([g["attn_" + n].T for n in ("Wq", "Wk", "Wv", "Wo")], axis=1)
    gate = np.concatenate([g["ffn_Wg_s"][None], g["ffn_Wg"]])
    up = np.concatenate([g["ffn_Wu_s"][None], g["ffn_Wu"]])
    down = np.concatenate([g["ffn_Wd_s"][None], g["ffn_Wd"]])
    gu = np.stack([gate, up], axis=1).reshape(SLOTS, 2, KC, P, FF).transpose(3, 0, 1, 2, 4)
    arrays = {
        "x": g["attn_x"],
        "w_qkvo": qkvo.reshape(KC, P, 4 * D).transpose(1, 0, 2),
        "w_gate_up": gu.reshape(P, SLOTS * 2 * KC * FF),
        "w_down": down.transpose(1, 0, 2).reshape(P, SLOTS * D),
        "w_router": g["ffn_gate_w"].T.reshape(KC, P, E).transpose(1, 0, 2),
        "bias": g["ffn_correction_bias"],
        "consts": constants(),
    }
    nc = bacc.Bacc("TRN2", target_bir_lowering=False, num_devices=1)
    ins, args = {}, []
    for name, v in arrays.items():
        v = np.ascontiguousarray(v)
        ins[f"in_{name}"] = v
        args.append(nc.dram_tensor(f"in_{name}", v.shape, mybir.dt.from_np(v.dtype), kind="ExternalInput").ap())
    args.append(nc.dram_tensor("out_y", (B, S, D), mybir.dt.float32, kind="ExternalOutput").ap())
    linear_attention_moe(nc, *args)
    r = run_bass_kernel_spmd(nc, [ins], core_ids=[0])
    return r.results[0]["out_y"]
```
